# Optimizing a Trainium2 kernel written in Bass

```python
import numpy as np
import jax
import jax.numpy as jnp

def _softmax(x, axis=-1):
    return jax.nn.softmax(x, axis=axis)

def _gelu(x):
    return jax.nn.gelu(x, approximate=True)

def _silu(x):
    return jax.nn.silu(x)

def _sigmoid(x):
    return jax.nn.sigmoid(x)

def _layernorm(x, axis=-1, eps=1e-05):
    m = jnp.mean(x, axis=axis, keepdims=True)
    v = jnp.var(x, axis=axis, keepdims=True)
    return (x - m) / jnp.sqrt(v + eps)

def _scatter_add(tgt, idx, src, axis=0):
    return tgt.at[idx].add(src)

def _segment_sum(src, seg, n):
    return jax.ops.segment_sum(src, seg, n)
kernel_name = 'mk_adj_preln_d4_adj_r2_d4028e'

def setup_inputs(seed: int=0):
    np.random.seed(seed)
    _w = jnp.asarray

    def _rec_inputs():
        import jax
        import jax.numpy as jnp
        _gk = jax.random.key(seed)
        x = -0.0005207 + 1.001 * jax.random.normal(jax.random.fold_in(_gk, 1), (3327, 256), jnp.float32)
        _a = jax.random.bernoulli(jax.random.fold_in(_gk, 2), 0.00961827, (3327, 3327))
        _af = _a.astype(jnp.float32)
        adj = _af
        return (x, adj)
    x, adj = _rec_inputs()

    def _L0_gnn_setup():
        import jax, jax.numpy as jnp
        import numpy as np
        ALPHA = 0.2
        NEG_INF = -1000000000000.0
        key = jax.random.key(seed)
        k1, k2, k3, k4, k5 = jax.random.split(key, 5)
        N, F = (2048, 256)
        inp = jax.random.normal(k1, (N, F), dtype=jnp.float32)
        adj = jax.random.randint(k2, (N, N), 0, 2).astype(jnp.float32)
        W = jax.random.normal(k3, (F, F), dtype=jnp.float32) * (1.414 / np.sqrt(F))
        a = jax.random.normal(k4, (2 * F, 1), dtype=jnp.float32) * 0.05
        wtrans = jax.random.normal(k5, (2 * F, F), dtype=jnp.float32) * (1.414 / np.sqrt(1.5 * F))
        return {'inp': inp, 'adj': adj, 'W': W, 'a': a, 'wtrans': wtrans}
    _L0_gnn_all = _L0_gnn_setup()
    _L0_gnn_in = {k: v for k, v in _L0_gnn_all.items() if k in ('W', 'a', 'wtrans')}
    del _L0_gnn_all

    def _L1_gnn_setup():
        import jax, jax.numpy as jnp
        import numpy as np
        N = 4096
        DIN = 256
        DOUT = 256
        key = jax.random.key(seed)
        k1, k2, k3 = jax.random.split(key, 3)
        x = jax.random.normal(k1, (N, DIN), dtype=jnp.float32)
        adj = jax.random.uniform(k2, (N, N), dtype=jnp.float32)
        W = jax.random.normal(k3, (DIN, DOUT), dtype=jnp.float32) * (1.0 / np.sqrt(DIN))
        b = jnp.zeros((DOUT,), dtype=jnp.float32)
        return {'x': x, 'adj': adj, 'W': W, 'b': b}
    _L1_gnn_all = _L1_gnn_setup()
    _L1_gnn_in = {k: v for k, v in _L1_gnn_all.items() if k in ('W', 'b')}
    del _L1_gnn_all

    def _L2_gnn_setup():
        import jax, jax.numpy as jnp
        import numpy as np

        def _bin_sign(v):
            return jnp.sign(v)

        def _bin_sign_z(v):
            return jnp.maximum(jnp.sign(v), 0.0)
        key = jax.random.key(seed)
        k1, k2, k3 = jax.random.split(key, 3)
        N, D_IN, D_OUT = (4096, 256, 256)
        x = jax.random.normal(k1, (N, D_IN), dtype=jnp.float32)
        support = jax.random.uniform(k2, (N, N), dtype=jnp.float32)
        weight = jax.random.normal(k3, (D_OUT, D_IN), dtype=jnp.float32)
        return {'x': x, 'support': support, 'weight': weight}
    _L2_gnn_all = _L2_gnn_setup()
    _L2_gnn_in = {k: v for k, v in _L2_gnn_all.items() if k in ('weight',)}
    del _L2_gnn_all

    def _L3_gnn_setup():
        import jax, jax.numpy as jnp
        import numpy as np
        N = 5000
        IN_F = 256
        OUT_F = 256
        key = jax.random.key(seed)
        k1, k2, k3 = jax.random.split(key, 3)
        x = jax.random.normal(k1, (N, IN_F), dtype=jnp.float32)
        adj = jax.random.uniform(k2, (N, N), dtype=jnp.float32)
        stdv = 1.0 / np.sqrt(OUT_F)
        weight = jax.random.uniform(k3, (IN_F, OUT_F), dtype=jnp.float32, minval=-stdv, maxval=stdv)
        t = jnp.ones((1,), dtype=jnp.float32)
        return {'x': x, 'adj': adj, 't': t, 'weight': weight}
    _L3_gnn_all = _L3_gnn_setup()
    _L3_gnn_in = {k: v for k, v in _L3_gnn_all.items() if k in ('t', 'weight')}
    del _L3_gnn_all
    return {'x': x, 'adj': adj, 'L0_gnn_W': _L0_gnn_in['W'], 'L0_gnn_a': _L0_gnn_in['a'], 'L0_gnn_wtrans': _L0_gnn_in['wtrans'], 'L1_gnn_W': _L1_gnn_in['W'], 'L1_gnn_b': _L1_gnn_in['b'], 'L2_gnn_weight': _L2_gnn_in['weight'], 'L3_gnn_t': _L3_gnn_in['t'], 'L3_gnn_weight': _L3_gnn_in['weight']}

def reference(x, adj, L0_gnn_W, L0_gnn_a, L0_gnn_wtrans, L1_gnn_W, L1_gnn_b, L2_gnn_weight, L3_gnn_t, L3_gnn_weight):
    import jax
    import jax.numpy as jnp

    def _L0_gnn_ref(inp, adj, W, a, wtrans):
        import jax, jax.numpy as jnp
        import numpy as np
        ALPHA = 0.2
        NEG_INF = -1000000000000.0
        F_out = W.shape[1]
        h = inp @ W
        Wh1 = h @ a[:F_out, :]
        Wh2 = h @ a[F_out:, :]
        e = jax.nn.leaky_relu(Wh1 + Wh2.T, ALPHA)
        mask = adj > 0
        attention = jax.nn.softmax(jnp.where(mask, e, NEG_INF), axis=1)
        negative_attention = -jax.nn.softmax(jnp.where(mask, -e, NEG_INF), axis=1)
        h_prime = attention @ inp
        h_prime_negative = negative_attention @ inp
        h_prime_double = jnp.concatenate([h_prime, h_prime_negative], axis=1)
        new_h_prime = h_prime_double @ wtrans
        return jax.nn.elu(new_h_prime)

    def _L1_gnn_ref(x, adj, W, b):
        import jax, jax.numpy as jnp
        import numpy as np
        N = 4096
        DIN = 256
        DOUT = 256
        rowsum = adj.sum(axis=1)
        d_inv_sqrt = jnp.where(rowsum > 0, rowsum ** (-0.5), 0.0)
        normalized_adj = d_inv_sqrt[:, None] * adj * d_inv_sqrt[None, :]
        support = normalized_adj @ x
        out = support @ W + b
        return jax.nn.relu(out)

    def _L2_gnn_ref(x, support, weight):
        import jax, jax.numpy as jnp
        import numpy as np

        def _bin_sign(v):
            return jnp.sign(v)

        def _bin_sign_z(v):
            return jnp.maximum(jnp.sign(v), 0.0)
        bw = _bin_sign(weight)
        ba = _bin_sign_z(x)
        xw = ba @ bw.T
        out = support @ xw
        return jax.nn.relu(out)

    def _L3_gnn_ref(x, adj, t, weight):
        import jax, jax.numpy as jnp
        import numpy as np
        N = 5000
        IN_F = 256
        OUT_F = 256
        ts = t[0]
        support = x @ weight
        return (1.0 - ts) * support + ts * (adj @ support)
    h = jnp.maximum(_layernorm(x, axis=-1), 0.0)
    x = x + _L0_gnn_ref(h, adj, L0_gnn_W, L0_gnn_a, L0_gnn_wtrans)
    h = jnp.maximum(_layernorm(x, axis=-1), 0.0)
    x = x + _L1_gnn_ref(h, adj, L1_gnn_W, L1_gnn_b)
    h = jnp.maximum(_layernorm(x, axis=-1), 0.0)
    x = x + _L2_gnn_ref(h, adj, L2_gnn_weight)
    h = jnp.maximum(_layernorm(x, axis=-1), 0.0)
    x = x + _L3_gnn_ref(h, adj, L3_gnn_t, L3_gnn_weight)
    return x

_drawn_inputs = setup_inputs


def setup_inputs(seed=0):
    import zlib

    import numpy as np

    out = dict(_drawn_inputs(seed))
    spreads = {'L1_gnn_b': (0.0, 0.1)}
    factors = {}
    for name, (base, spread) in spreads.items():
        noise = np.random.default_rng([zlib.crc32(name.encode()), seed]).standard_normal(out[name].shape)
        drawn = base * np.exp(spread * noise) if base else spread * noise
        out[name] = jnp.asarray(drawn.astype(out[name].dtype))
    for name, factor in factors.items():
        out[name] = (out[name] * factor).astype(out[name].dtype)
    return out
```

```python
from contextlib import ExitStack

import numpy as np
import concourse.bass as bass
from concourse import mybir

P = 128
F32 = mybir.dt.float32
ALU = mybir.AluOpType
ACT = mybir.ActivationFunctionType
AX = mybir.AxisListType

N, F = 3327, 256
TILES = -(-N // P)
NP = TILES * P
PAIRS = TILES // 2
FB = F // P
ALPHA = 0.2
MASKED = 1e12
EPS = 1e-5
GROUPS = [(g, min(4, TILES - g)) for g in range(0, TILES, 4)]


def gnn_program(nc, x_by_part, adj, adj_t, w_att_t, a_vec, wtrans, w1, b1, w2_t, t3, w3, ident_in, out):
    with ExitStack() as ctx:
        def sb(name, shape, dt=F32):
            return ctx.enter_context(nc.sbuf_tensor(name, shape, dt))

        def ps(name):
            return ctx.enter_context(nc.psum_tensor(name, [P, 512], F32))

        def sem(name):
            return ctx.enter_context(nc.semaphore(name))

        xs = sb("xs", [P, TILES, F])
        h = sb("h", [P, TILES, F])
        ident = sb("ident", [P, P])
        ones = sb("ones", [P, P])
        w_att_sb = sb("w_att_sb", [P, FB, F])
        a_sb = sb("a_sb", [P, 2, FB])
        wtrans_sb = sb("wtrans_sb", [P, 2 * FB, F])
        w_sb = {1: sb("w1_sb", [P, FB, F]), 2: sb("w2_sb", [P, FB, F]), 3: sb("w3_sb", [P, FB, F])}
        b_row = sb("b_row", [P, F])
        t_col = sb("t_col", [P, 1])
        omt_col = sb("omt_col", [P, 1])
        wa = sb("wa", [P, 2, F])
        s_col = sb("s_col", [P, TILES])
        t_nodes = sb("t_nodes", [P, TILES])
        t_row = sb("t_row", [P, NP])
        rowsum = sb("rowsum", [P, TILES])
        stats = sb("stats", [P, TILES, 6])
        mean = sb("mean", [P, TILES])
        var = sb("var", [P, TILES])
        rec = sb("rec", [P, TILES])
        rstd = sb("rstd", [P, TILES])
        nwt = sb("nwt", [P, TILES])
        dinv = sb("dinv", [P, TILES])
        diag = sb("diag", [P, 2, P])
        abuf = sb("abuf", [P, 2, NP])
        ebuf = sb("ebuf", [P, NP])
        prob = sb("prob", [P, NP])
        prob_t = sb("prob_t", [P, TILES, P])
        nmax = sb("nmax", [P, 2])
        psums = sb("psums", [P, 2])
        prec = sb("prec", [P, 2])
        y_sb = sb("y_sb", [P, 2 * F])
        yt_sb = sb("yt_sb", [P, 2 * F])
        elu_m = sb("elu_m", [P, F])
        elu_e = sb("elu_e", [P, F])

        tp = [ps(f"tp{i}") for i in range(2)]
        yp = [ps(f"yp{i}") for i in range(2)]
        ep = [ps(f"ep{i}") for i in range(2)]
        op = [ps(f"op{i}") for i in range(2)]

        loaded = sem("loaded")
        prep = sem("prep")
        wa_done = sem("wa_done")
        wa_here = sem("wa_here")
        with nc.Block() as block:
            @block.sync
            def _(sp):
                sp.dma_start(xs[:], x_by_part).then_inc(loaded, 16)
                sp.dma_start(ident[:], ident_in).then_inc(loaded, 16)
                sp.dma_start(w_att_sb[:], w_att_t.rearrange("(c p) f -> p c f", p=P)).then_inc(loaded, 16)
                sp.dma_start(a_sb[:], a_vec.rearrange("p (s c) -> p s c", s=2)).then_inc(loaded, 16)
                sp.dma_start(wtrans_sb[:], wtrans.rearrange("(c p) f -> p c f", p=P)).then_inc(loaded, 16)
                for layer, w in ((1, w1), (2, w2_t), (3, w3)):
                    sp.dma_start(w_sb[layer][:], w.rearrange("(c p) f -> p c f", p=P)).then_inc(loaded, 16)
                sp.dma_start(b_row[:], b1.rearrange("(a f) -> a f", a=1).broadcast_to([P, F])).then_inc(loaded, 16)
                sp.dma_start(t_col[:], t3.rearrange("(a f) -> a f", a=1).broadcast_to([P, 1])).then_inc(loaded, 16)

            @block.vector
            def _(v):
                v.memset(ones[:], 1.0).then_inc(prep, 1)
                v.memset(prob[:], 0.0).then_inc(prep, 1)
                v.wait_ge(loaded, 160)
                v.wait_ge(prep, 2)
                rep = prob[:, 0:2 * FB * P].rearrange("p (s c m) -> p s c m", s=2, c=FB)
                for s in range(2):
                    for c in range(FB):
                        v.tensor_scalar(rep[:, s, c, :], ones[:], a_sb[:, s, c:c + 1], None,
                                        ALU.mult).then_inc(prep, 1)
                w2v = w_sb[2][:]
                v.tensor_scalar(h[:, 0:FB, :], w2v, 0.0, None, ALU.is_gt).then_inc(prep, 1)
                v.tensor_scalar(h[:, FB:2 * FB, :], w2v, 0.0, None, ALU.is_lt).then_inc(prep, 1)
                v.wait_ge(prep, 8)
                v.tensor_tensor(w2v, h[:, 0:FB, :], h[:, FB:2 * FB, :], ALU.subtract).then_inc(prep, 1)
                v.tensor_scalar(omt_col[:], t_col[:], -1.0, 1.0, ALU.mult, ALU.add).then_inc(prep, 1)
                v.wait_ge(wa_done, 1)
                v.tensor_copy(wa[:], yp[0][:].rearrange("p (s f) -> p s f", s=2)).then_inc(wa_here, 1)
                v.memset(prob[:, 0:2 * FB * P], 0.0).then_inc(wa_here, 1)

            @block.tensor
            def _(pe):
                pe.wait_ge(prep, 6)
                rep = prob[:, 0:2 * FB * P].rearrange("p (s c m) -> p s c m", s=2, c=FB)
                for s in range(2):
                    for c in range(FB):
                        mm = pe.matmul(yp[0][:, s * F:(s + 1) * F], rep[:, s, c, :], w_att_sb[:, c, :],
                                       start=(c == 0), stop=(c == FB - 1))
                mm.then_inc(wa_done, 1)

        def layer_norm(layer):
            lv = sem(f"ln_v{layer}")
            la = sem(f"ln_a{layer}")
            lp = sem(f"ln_p{layer}")
            with nc.Block() as block:
                @block.vector
                def _(v):
                    with v.Fori(0, TILES) as t:
                        v.bn_stats(stats[:, bass.ds(t, 1), :], xs[:, bass.ds(t, 1), :]).then_inc(lv, 1)
                    n = TILES

                    def step(inst, n):
                        inst.then_inc(lv, 1)
                        v.wait_ge(lv, n + 1)
                        return n + 1
                    v.wait_ge(lv, n)

                    def rsqrt(o, i, roots, n):
                        n = step(v.reciprocal(rec[:], i), n)
                        v.wait_ge(la, roots)
                        n = step(v.tensor_tensor(nwt[:], o, o, ALU.mult), n)
                        n = step(v.tensor_tensor(nwt[:], nwt[:], i, ALU.mult), n)
                        n = step(v.tensor_scalar(nwt[:], nwt[:], -0.5, 1.5, ALU.mult, ALU.add), n)
                        return step(v.tensor_tensor(o, o, nwt[:], ALU.mult), n)
                    n = step(v.tensor_tensor(mean[:], stats[:, :, 1], stats[:, :, 4], ALU.add), n)
                    n = step(v.tensor_scalar(mean[:], mean[:], 0.5, None, ALU.mult), n)
                    n = step(v.tensor_tensor(rec[:], stats[:, :, 1], stats[:, :, 4], ALU.subtract), n)
                    n = step(v.scalar_tensor_tensor(rec[:], rec[:], 0.25, rec[:], ALU.mult, ALU.mult), n)
                    n = step(v.tensor_tensor(var[:], stats[:, :, 2], stats[:, :, 5], ALU.add), n)
                    n = step(v.scalar_tensor_tensor(var[:], var[:], 1.0 / F, rec[:], ALU.mult, ALU.add), n)
                    n = step(v.tensor_scalar(var[:], var[:], EPS, None, ALU.add), n)
                    n = rsqrt(rstd[:], var[:], 1, n)
                    if layer == 1:
                        n = step(v.tensor_scalar(var[:], rowsum[:], 1e-34, None, ALU.max), n)
                        n = rsqrt(dinv[:], var[:], 2, n)
                        n = step(v.tensor_scalar(nwt[:], rowsum[:], 0.0, None, ALU.is_gt), n)
                        n = step(v.tensor_tensor(dinv[:], dinv[:], nwt[:], ALU.mult), n)
                        n = step(v.tensor_tensor(rstd[:], rstd[:], dinv[:], ALU.mult), n)
                    with v.Fori(0, TILES) as t:
                        ht = h[:, bass.ds(t, 1), :]
                        xt = xs[:, bass.ds(t, 1), :]
                        m = mean[:, bass.ds(t, 1)]
                        if layer == 2:
                            v.tensor_scalar(ht, xt, m, None, ALU.is_gt).then_inc(lv, 1)
                        else:
                            v.tensor_scalar(ht, xt, m, 0.0, ALU.subtract, ALU.max).then_inc(lv, 1)
                            v.wait_ge(lv, n + 1 + t * (4 if layer == 0 else 2))
                            v.tensor_scalar(ht, ht, rstd[:, bass.ds(t, 1)], None, ALU.mult).then_inc(lv, 1)
                        if layer == 0:
                            for s, o in enumerate((s_col, t_nodes)):
                                v.wait_ge(lv, n + 2 + s + t * 4)
                                v.scalar_tensor_tensor(ebuf[:, 0:F], h[:, bass.ds(t, 1), :].rearrange("p a f -> p (a f)"),
                                                       1.0, wa[:, s, :], ALU.mult, ALU.mult,
                                                       accum_out=o[:, bass.ds(t, 1)]).then_inc(lv, 1)
                    if layer == 0:
                        n += 4 * TILES
                        for t in range(TILES):
                            v.wait_ge(lv, n)
                            if t >= 2:
                                v.wait_ge(lp, t - 1)
                            v.tensor_scalar(diag[:, t % 2, :], ident[:], t_nodes[:, t:t + 1], None,
                                            ALU.mult).then_inc(la, 1)
                            if t >= 1:
                                v.wait_ge(lp, t)
                                v.tensor_copy(t_row[:, (t - 1) * P:t * P], tp[(t - 1) % 2][:, 0:P]).then_inc(wa_here, 1)
                        v.wait_ge(lp, TILES)
                        v.tensor_copy(t_row[:, (TILES - 1) * P:], tp[(TILES - 1) % 2][:, 0:P]).then_inc(wa_here, 1)

                @block.scalar
                def _(a):
                    n = TILES + 7
                    a.wait_ge(lv, n + 1)
                    a.activation(rstd[:], rec[:], ACT.Sqrt).then_inc(la, 1)
                    if layer == 1:
                        a.wait_ge(lv, n + 7)
                        a.activation(dinv[:], rec[:], ACT.Sqrt).then_inc(la, 1)

                if layer == 0:
                    @block.tensor
                    def _(pe):
                        for t in range(TILES):
                            pe.wait_ge(la, 2 + t)
                            if t >= 2:
                                pe.wait_ge(wa_here, 2 + t - 1)
                            pe.matmul(tp[t % 2][:, 0:P], ones[:], diag[:, t % 2, :],
                                      start=True, stop=True).then_inc(lp, 1)

        layer_norm(0)

        a_here = [sem(f"a_here{p}") for p in range(2)]
        a_free = [sem(f"a_free{p}") for p in range(2)]
        vq = sem("vq")
        expd = sem("expd")
        tpd = sem("tpd")
        tpc = sem("tpc")
        ypd = sem("ypd")
        epd = sem("epd")
        epc = sem("epc")
        opd = sem("opd")
        elu = sem("elu")
        NG = len(GROUPS)
        VT = 17
        with nc.Block() as block:
            @block.sync
            def _(sp):
                with sp.Fori(0, PAIRS) as k:
                    for p in range(2):
                        t = 2 * k + p
                        sp.wait_ge(a_free[p], k + 1)
                        sp.dma_start(abuf[:, p, :], adj[bass.ds(t * P, P), :]).then_inc(a_here[p], 16)

            @block.vector
            def _(v):
                for p in range(2):
                    v.nop().then_inc(a_free[p], 1)
                with v.Fori(0, PAIRS) as k:
                    for p in range(2):
                        t = 2 * k + p
                        base = t * VT
                        ab = abuf[:, p, :]

                        def step(inst, n):
                            inst.then_inc(vq, 1)
                            v.wait_ge(vq, base + n)
                        v.wait_ge(a_here[p], 16 * k + 16)
                        v.tensor_reduce(rowsum[:, bass.ds(t, 1)], ab, AX.X, ALU.add).then_inc(vq, 1)
                        step(v.tensor_scalar(ebuf[:], t_row[:], s_col[:, bass.ds(t, 1)], None, ALU.add), 2)
                        step(v.tensor_scalar(ab, ab, 0.0, None, ALU.is_gt), 3)
                        step(v.scalar_tensor_tensor(ebuf[:], ebuf[:], ALPHA, ebuf[:], ALU.mult, ALU.max), 4)
                        step(v.tensor_tensor(ebuf[:], ebuf[:], ab, ALU.mult), 5)
                        step(v.tensor_scalar(ab, ab, 1.0, MASKED, ALU.subtract, ALU.mult), 6)
                        v.wait_ge(tpd, 1 + 2 * NG * t)
                        step(v.tensor_tensor(prob[:, 0:N], ebuf[:, 0:N], ab[:, 0:N], ALU.add), 7)
                        v.tensor_reduce(nmax[:, 0:1], prob[:, 0:N], AX.X, ALU.max, negate=True).then_inc(vq, 1)
                        v.wait_ge(tpd, 1 + 2 * NG * t + NG)
                        step(v.scalar_tensor_tensor(prob[:, 0:N], ebuf[:, 0:N], -1.0, ab[:, 0:N], ALU.mult, ALU.add), 9)
                        v.tensor_reduce(nmax[:, 1:2], prob[:, 0:N], AX.X, ALU.max, negate=True).then_inc(a_free[p], 1)
                        v.wait_ge(expd, 2 * t + 2)
                        step(v.reciprocal(prec[:], psums[:]), 10)
                        step(v.tensor_scalar(prec[:, 1:2], prec[:, 1:2], -1.0, None, ALU.mult), 11)
                        v.wait_ge(ypd, 1 + 2 * t + 2)
                        for s in range(2):
                            v.tensor_scalar(y_sb[:, s * F:(s + 1) * F], yp[s][:, 0:F], prec[:, s:s + 1], None,
                                            ALU.mult).then_inc(vq, 1)
                        v.wait_ge(opd, t + 1)
                        v.tensor_scalar(elu_m[:], op[0][:, 0:F], 0.0, None, ALU.min).then_inc(vq, 1)
                        v.wait_ge(elu, t + 1)
                        v.tensor_scalar(elu_e[:], elu_e[:], -1.0, None, ALU.add).then_inc(vq, 1)
                        v.wait_ge(vq, base + 15)
                        v.scalar_tensor_tensor(elu_e[:], op[0][:, 0:F], 0.0, elu_e[:], ALU.max, ALU.add).then_inc(vq, 1)
                        v.wait_ge(vq, base + 16)
                        xt = xs[:, bass.ds(t, 1), :].rearrange("p a f -> p (a f)")
                        v.tensor_tensor(xt, xt, elu_e[:], ALU.add).then_inc(vq, 1)

            @block.scalar
            def _(a):
                with a.Fori(0, PAIRS) as k:
                    for p in range(2):
                        t = 2 * k + p
                        for s in range(2):
                            if s == 0:
                                a.wait_ge(vq, VT * t + 8)
                            else:
                                a.wait_ge(a_free[p], k + 2)
                            a.activation(prob[:, 0:N], prob[:, 0:N], ACT.Exp, bias=nmax[:, s:s + 1],
                                         accum_out=psums[:, s:s + 1]).then_inc(expd, 1)
                            for g, (j, n) in enumerate(GROUPS):
                                a.wait_ge(tpd, 1 + (2 * t + s) * NG + g + 1)
                                if g == 0:
                                    a.wait_ge(ypd, 1 + 2 * t + s)
                                a.activation(prob_t[:, j:j + n, :], tp[(s * NG + g) % 2][:, 0:n * P].rearrange("p (j i) -> p j i", j=n), ACT.Copy)\
                                 .then_inc(tpc, 1)
                        a.wait_ge(epd, t + 1)
                        a.activation(yt_sb[:], ep[0][:], ACT.Copy).then_inc(epc, 1)
                        a.wait_ge(vq, VT * t + 14)
                        a.activation(elu_e[:], elu_m[:], ACT.Exp).then_inc(elu, 1)

            @block.tensor
            def _(pe):
                pe.nop().then_inc(tpd, 1)
                pe.nop().then_inc(ypd, 1)
                with pe.Fori(0, PAIRS) as k:
                    for p in range(2):
                        t = 2 * k + p
                        for s in range(2):
                            pe.wait_ge(expd, 2 * t + s + 1)
                            for g, (j, n) in enumerate(GROUPS):
                                q = (2 * p + s) * NG + g
                                if q >= 2:
                                    pe.wait_ge(tpc, 4 * NG * k + q - 1)
                                for i in range(n):
                                    tr = pe.transpose(tp[(s * NG + g) % 2][:, i * P:(i + 1) * P],
                                                      prob[:, (j + i) * P:(j + i + 1) * P], ident[:])
                                tr.then_inc(tpd, 1)
                            pe.wait_ge(tpc, (2 * t + s + 1) * NG)
                            for j in range(TILES):
                                mm = pe.matmul(yp[s][:, 0:F], prob_t[:, j, :], h[:, j, :],
                                               start=(j == 0), stop=(j == TILES - 1))
                            mm.then_inc(ypd, 1)
                        pe.wait_ge(vq, VT * t + 13)
                        for c in range(2 * FB):
                            tr = pe.transpose(ep[0][:, c * P:(c + 1) * P], y_sb[:, c * P:(c + 1) * P], ident[:])
                        tr.then_inc(epd, 1)
                        pe.wait_ge(epc, t + 1)
                        for c in range(2 * FB):
                            mm = pe.matmul(op[0][:, 0:F], yt_sb[:, c * P:(c + 1) * P], wtrans_sb[:, c, :],
                                           start=(c == 0), stop=(c == 2 * FB - 1))
                        mm.then_inc(opd, 1)

        def graph_layer(layer):
            b_here = [sem(f"b_here{layer}_{p}") for p in range(2)]
            y_done = [sem(f"y_done{layer}_{p}") for p in range(2)]
            y_here = [sem(f"y_here{layer}_{p}") for p in range(2)]
            z_done = sem(f"z_done{layer}")
            zt_done = sem(f"zt_done{layer}")
            zt_here = sem(f"zt_here{layer}")
            o_done = sem(f"o_done{layer}")
            v_done = sem(f"v_done{layer}")
            with nc.Block() as block:
                @block.sync
                def _(sp):
                    with sp.Fori(0, PAIRS) as k:
                        for p in range(2):
                            t = 2 * k + p
                            sp.wait_ge(y_done[p], k + 1)
                            sp.dma_start(abuf[:, p, :], adj_t[bass.ds(t * P, P), :]).then_inc(b_here[p], 16)

                @block.tensor
                def _(pe):
                    for p in range(2):
                        pe.nop().then_inc(y_done[p], 1)
                    with pe.Fori(0, PAIRS) as k:
                        for p in range(2):
                            t = 2 * k + p
                            pe.wait_ge(b_here[p], 16 * k + 16)
                            pe.wait_ge(y_here[p], k + 1)
                            for j in range(TILES):
                                mm = pe.matmul(yp[p][:, 0:F], abuf[:, p, j * P:(j + 1) * P], h[:, j, :],
                                               start=(j == 0), stop=(j == TILES - 1))
                            mm.then_inc(y_done[p], 1)
                            pe.wait_ge(z_done, t + 1)
                            for c in range(FB):
                                tr = pe.transpose(ep[p][:, c * P:(c + 1) * P], y_sb[:, p * F + c * P:p * F + (c + 1) * P], ident[:])
                            tr.then_inc(zt_done, 1)
                            pe.wait_ge(zt_here, t + 1)
                            for c in range(FB):
                                mm = pe.matmul(op[p][:, 0:F], yt_sb[:, p * F + c * P:p * F + (c + 1) * P], w_sb[layer][:, c, :],
                                               start=(c == 0), stop=(c == FB - 1))
                            mm.then_inc(o_done, 1)

                @block.scalar
                def _(a):
                    with a.Fori(0, PAIRS) as k:
                        for p in range(2):
                            t = 2 * k + p
                            a.wait_ge(zt_done, t + 1)
                            a.activation(yt_sb[:, p * F:(p + 1) * F], ep[p][:, 0:F], ACT.Copy).then_inc(zt_here, 1)

                @block.vector
                def _(v):
                    for p in range(2):
                        v.nop().then_inc(y_here[p], 1)
                    with v.Fori(0, PAIRS) as k:
                        for p in range(2):
                            t = 2 * k + p
                            y, z = yp[p][:, 0:F], y_sb[:, p * F:(p + 1) * F]
                            xt = xs[:, bass.ds(t, 1), :].rearrange("p a f -> p (a f)")
                            ht = h[:, bass.ds(t, 1), :].rearrange("p a f -> p (a f)")
                            v.wait_ge(y_done[p], k + 2)
                            if layer == 1:
                                v.tensor_scalar(z, y, dinv[:, bass.ds(t, 1)], None, ALU.mult).then_inc(z_done, 1)
                                v.nop().then_inc(y_here[p], 1)
                            elif layer == 2:
                                v.tensor_copy(z, y).then_inc(z_done, 1)
                                v.nop().then_inc(y_here[p], 1)
                            else:
                                v.tensor_scalar(elu_m[:], y, t_col[:], None, ALU.mult).then_inc(y_here[p], 1)
                                v.wait_ge(y_here[p], k + 2)
                                v.scalar_tensor_tensor(z, ht, omt_col[:], elu_m[:], ALU.mult, ALU.add).then_inc(z_done, 1)
                            v.wait_ge(o_done, t + 1)
                            if layer == 1:
                                v.tensor_tensor(elu_e[:], op[p][:, 0:F], b_row[:], ALU.add).then_inc(v_done, 1)
                                v.wait_ge(v_done, 2 * t + 1)
                                v.scalar_tensor_tensor(xt, elu_e[:], 0.0, xt, ALU.max, ALU.add).then_inc(v_done, 1)
                            elif layer == 2:
                                v.scalar_tensor_tensor(xt, op[p][:, 0:F], 0.0, xt, ALU.max, ALU.add).then_inc(v_done, 1)
                            else:
                                v.tensor_tensor(xt, op[p][:, 0:F], xt, ALU.add).then_inc(v_done, 1)

        for layer in (1, 2, 3):
            layer_norm(layer)
            graph_layer(layer)

        stored = sem("stored")
        with nc.Block() as block:
            @block.sync
            def _(sp):
                full = (TILES - 1) * P
                sp.dma_start(out[0:full, :].rearrange("(t p) f -> p t f", p=P), xs[:, 0:TILES - 1, :]).then_inc(stored, 16)
                sp.dma_start(out[full:N, :], xs[0:N - full, TILES - 1, :]).then_inc(stored, 16)
                sp.wait_ge(stored, 32)


def kernel(x, adj, L0_gnn_W, L0_gnn_a, L0_gnn_wtrans, L1_gnn_W, L1_gnn_b, L2_gnn_weight, L3_gnn_t, L3_gnn_weight):
    import concourse.bacc as bacc
    from concourse.bass_utils import run_bass_kernel_spmd

    adj_pad = np.pad(np.asarray(adj), ((0, NP - N), (0, NP - N)))
    x_pad = np.pad(np.asarray(x), ((0, NP - N), (0, 0)))
    arrays = {
        "x_by_part": np.ascontiguousarray(x_pad.reshape(TILES, P, F).transpose(1, 0, 2)),
        "adj": adj_pad,
        "adj_t": np.ascontiguousarray(
            adj_pad.reshape(TILES, P, TILES, P).transpose(0, 3, 2, 1).reshape(NP, NP)),
        "w_att_t": np.ascontiguousarray(np.asarray(L0_gnn_W).T),
        "a_vec": np.ascontiguousarray(np.asarray(L0_gnn_a).reshape(2 * FB, P).T),
        "wtrans": np.asarray(L0_gnn_wtrans),
        "w1": np.asarray(L1_gnn_W),
        "b1": np.asarray(L1_gnn_b),
        "w2_t": np.ascontiguousarray(np.asarray(L2_gnn_weight).T),
        "t3": np.asarray(L3_gnn_t),
        "w3": np.asarray(L3_gnn_weight),
        "ident": np.eye(P, dtype=np.float32),
    }
    nc = bacc.Bacc("TRN2", target_bir_lowering=False, num_devices=1)
    aps = [nc.dram_tensor(n + "_dram", a.shape, mybir.dt.from_np(a.dtype), kind="ExternalInput").ap()
           for n, a in arrays.items()]
    out = nc.dram_tensor("out_dram", (N, F), F32, kind="ExternalOutput").ap()
    gnn_program(nc, *aps, out)
    r = run_bass_kernel_spmd(nc, [{n + "_dram": a for n, a in arrays.items()}], core_ids=[0])
    return r.results[0]["out_dram"]
```

```python
from contextlib import ExitStack

import numpy as np
import concourse.bass as bass
from concourse import mybir

P = 128
F32 = mybir.dt.float32
F16 = mybir.dt.float16
F8 = mybir.dt.float8e4
U8 = mybir.dt.uint8
I32 = mybir.dt.int32
ALU = mybir.AluOpType
ACT = mybir.ActivationFunctionType
AX = mybir.AxisListType

N, F = 3327, 256
TILES = -(-N // P)
NP = TILES * P
PAIRS = TILES // 2
FB = F // P
ALPHA = 0.2
MASKED = 1e12
EPS = 1e-5
SPREAD = 10.0
SCALE = 2048.0
TINY = 1e-30
GROUPS = [(g, min(4, TILES - g)) for g in range(0, TILES, 4)]


def general_program(nc, io, prefix="g_"):
    adj, adj_t, w_att_t, a_vec, wtrans, w1, b1, w2_t, t3, w3, out = (
        io[n] for n in ("adj", "adj_t", "w_att_t", "a_vec", "wtrans", "w1", "b1", "w2_t", "t3", "w3", "out"))
    with ExitStack() as ctx:
        def sb(name, shape, dt=F32):
            return ctx.enter_context(nc.sbuf_tensor(prefix + name, shape, dt))

        def ps(name):
            return ctx.enter_context(nc.psum_tensor(prefix + name, [P, 512], F32))

        def sem(name):
            return ctx.enter_context(nc.semaphore(prefix + name))

        xs = sb("xs", [P, TILES, F])
        h = sb("h", [P, TILES, F])
        ident = sb("ident", [P, P])
        ones = sb("ones", [P, P])
        w_att_sb = sb("w_att_sb", [P, FB, F])
        a_sb = sb("a_sb", [P, 2, FB])
        wtrans_sb = sb("wtrans_sb", [P, 2 * FB, F])
        w_sb = {1: sb("w1_sb", [P, FB, F]), 2: sb("w2_sb", [P, FB, F]), 3: sb("w3_sb", [P, FB, F])}
        b_row = sb("b_row", [P, F])
        t_col = sb("t_col", [P, 1])
        omt_col = sb("omt_col", [P, 1])
        wa = sb("wa", [P, 2, F])
        s_col = sb("s_col", [P, TILES])
        t_nodes = sb("t_nodes", [P, TILES])
        t_row = sb("t_row", [P, NP])
        rowsum = sb("rowsum", [P, TILES])
        stats = sb("stats", [P, TILES, 6])
        mean = sb("mean", [P, TILES])
        var = sb("var", [P, TILES])
        rec = sb("rec", [P, TILES])
        rstd = sb("rstd", [P, TILES])
        nwt = sb("nwt", [P, TILES])
        dinv = sb("dinv", [P, TILES])
        diag = sb("diag", [P, 2, P])
        abuf = sb("abuf", [P, 2, NP])
        ebuf = sb("ebuf", [P, NP])
        prob = sb("prob", [P, NP])
        prob_t = sb("prob_t", [P, TILES, P])
        nmax = sb("nmax", [P, 2])
        psums = sb("psums", [P, 2])
        prec = sb("prec", [P, 2])
        y_sb = sb("y_sb", [P, 2 * F])
        yt_sb = sb("yt_sb", [P, 2 * F])
        elu_m = sb("elu_m", [P, F])
        elu_e = sb("elu_e", [P, F])

        tp = [ps(f"tp{i}") for i in range(2)]
        yp = [ps(f"yp{i}") for i in range(2)]
        ep = [ps(f"ep{i}") for i in range(2)]
        op = [ps(f"op{i}") for i in range(2)]

        loaded = sem("loaded")
        prep = sem("prep")
        wa_done = sem("wa_done")
        wa_here = sem("wa_here")
        with nc.Block() as block:
            @block.sync
            def _(sp):
                sp.dma_start(xs[:], io["x"]).then_inc(loaded, 16)
                sp.dma_start(ident[:], io["ident"]).then_inc(loaded, 16)
                sp.dma_start(w_att_sb[:], w_att_t.rearrange("(c p) f -> p c f", p=P)).then_inc(loaded, 16)
                sp.dma_start(a_sb[:], a_vec.rearrange("p (s c) -> p s c", s=2)).then_inc(loaded, 16)
                sp.dma_start(wtrans_sb[:], wtrans.rearrange("(c p) f -> p c f", p=P)).then_inc(loaded, 16)
                for layer, w in ((1, w1), (2, w2_t), (3, w3)):
                    sp.dma_start(w_sb[layer][:], w.rearrange("(c p) f -> p c f", p=P)).then_inc(loaded, 16)

            @block.scalar
            def _(a):
                a.dma_start(b_row[:], b1.rearrange("(a f) -> a f", a=1).broadcast_to([P, F])).then_inc(loaded, 16)
                a.dma_start(t_col[:], t3.rearrange("(a f) -> a f", a=1).broadcast_to([P, 1])).then_inc(loaded, 16)

            @block.gpsimd
            def _(g):
                g.memset(ones[:], 1.0).then_inc(prep, 1)

            @block.vector
            def _(v):
                v.memset(prob[:], 0.0).then_inc(prep, 1)
                v.wait_ge(loaded, 160)
                v.wait_ge(prep, 2)
                rep = prob[:, 0:2 * FB * P].rearrange("p (s c m) -> p s c m", s=2, c=FB)
                for s in range(2):
                    for c in range(FB):
                        v.tensor_scalar(rep[:, s, c, :], ones[:], a_sb[:, s, c:c + 1], None,
                                        ALU.mult).then_inc(prep, 1)
                w2v = w_sb[2][:]
                v.tensor_scalar(h[:, 0:FB, :], w2v, 0.0, None, ALU.is_gt).then_inc(prep, 1)
                v.tensor_scalar(h[:, FB:2 * FB, :], w2v, 0.0, None, ALU.is_lt).then_inc(prep, 1)
                v.wait_ge(prep, 8)
                v.tensor_tensor(w2v, h[:, 0:FB, :], h[:, FB:2 * FB, :], ALU.subtract).then_inc(prep, 1)
                v.tensor_scalar(omt_col[:], t_col[:], -1.0, 1.0, ALU.mult, ALU.add).then_inc(prep, 1)
                v.wait_ge(wa_done, 1)
                v.tensor_copy(wa[:], yp[0][:].rearrange("p (s f) -> p s f", s=2)).then_inc(wa_here, 1)
                v.memset(prob[:, 0:2 * FB * P], 0.0).then_inc(wa_here, 1)

            @block.tensor
            def _(pe):
                pe.wait_ge(prep, 6)
                rep = prob[:, 0:2 * FB * P].rearrange("p (s c m) -> p s c m", s=2, c=FB)
                for s in range(2):
                    for c in range(FB):
                        mm = pe.matmul(yp[0][:, s * F:(s + 1) * F], rep[:, s, c, :], w_att_sb[:, c, :],
                                       start=(c == 0), stop=(c == FB - 1))
                mm.then_inc(wa_done, 1)

        def layer_norm(layer):
            lv = sem(f"ln_v{layer}")
            la = sem(f"ln_a{layer}")
            lp = sem(f"ln_p{layer}")
            with nc.Block() as block:
                @block.vector
                def _(v):
                    with v.Fori(0, TILES) as t:
                        v.bn_stats(stats[:, bass.ds(t, 1), :], xs[:, bass.ds(t, 1), :]).then_inc(lv, 1)
                    n = TILES

                    def step(inst, n):
                        inst.then_inc(lv, 1)
                        v.wait_ge(lv, n + 1)
                        return n + 1
                    v.wait_ge(lv, n)

                    def rsqrt(o, i, roots, n):
                        n = step(v.reciprocal(rec[:], i), n)
                        v.wait_ge(la, roots)
                        n = step(v.tensor_tensor(nwt[:], o, o, ALU.mult), n)
                        n = step(v.tensor_tensor(nwt[:], nwt[:], i, ALU.mult), n)
                        n = step(v.tensor_scalar(nwt[:], nwt[:], -0.5, 1.5, ALU.mult, ALU.add), n)
                        return step(v.tensor_tensor(o, o, nwt[:], ALU.mult), n)
                    n = step(v.tensor_tensor(mean[:], stats[:, :, 1], stats[:, :, 4], ALU.add), n)
                    n = step(v.tensor_scalar(mean[:], mean[:], 0.5, None, ALU.mult), n)
                    n = step(v.tensor_tensor(rec[:], stats[:, :, 1], stats[:, :, 4], ALU.subtract), n)
                    n = step(v.scalar_tensor_tensor(rec[:], rec[:], 0.25, rec[:], ALU.mult, ALU.mult), n)
                    n = step(v.tensor_tensor(var[:], stats[:, :, 2], stats[:, :, 5], ALU.add), n)
                    n = step(v.scalar_tensor_tensor(var[:], var[:], 1.0 / F, rec[:], ALU.mult, ALU.add), n)
                    n = step(v.tensor_scalar(var[:], var[:], EPS, None, ALU.add), n)
                    n = rsqrt(rstd[:], var[:], 1, n)
                    if layer == 1:
                        n = step(v.tensor_scalar(var[:], rowsum[:], 1e-34, None, ALU.max), n)
                        n = rsqrt(dinv[:], var[:], 2, n)
                        n = step(v.tensor_scalar(nwt[:], rowsum[:], 0.0, None, ALU.is_gt), n)
                        n = step(v.tensor_tensor(dinv[:], dinv[:], nwt[:], ALU.mult), n)
                        n = step(v.tensor_tensor(rstd[:], rstd[:], dinv[:], ALU.mult), n)
                    with v.Fori(0, TILES) as t:
                        ht = h[:, bass.ds(t, 1), :]
                        xt = xs[:, bass.ds(t, 1), :]
                        m = mean[:, bass.ds(t, 1)]
                        if layer == 2:
                            v.tensor_scalar(ht, xt, m, None, ALU.is_gt).then_inc(lv, 1)
                        else:
                            v.tensor_scalar(ht, xt, m, 0.0, ALU.subtract, ALU.max).then_inc(lv, 1)
                            v.wait_ge(lv, n + 1 + t * (4 if layer == 0 else 2))
                            v.tensor_scalar(ht, ht, rstd[:, bass.ds(t, 1)], None, ALU.mult).then_inc(lv, 1)
                        if layer == 0:
                            for s, o in enumerate((s_col, t_nodes)):
                                v.wait_ge(lv, n + 2 + s + t * 4)
                                v.scalar_tensor_tensor(ebuf[:, 0:F], h[:, bass.ds(t, 1), :].rearrange("p a f -> p (a f)"),
                                                       1.0, wa[:, s, :], ALU.mult, ALU.mult,
                                                       accum_out=o[:, bass.ds(t, 1)]).then_inc(lv, 1)
                    if layer == 0:
                        n += 4 * TILES
                        for t in range(TILES):
                            v.wait_ge(lv, n)
                            if t >= 2:
                                v.wait_ge(lp, t - 1)
                            v.tensor_scalar(diag[:, t % 2, :], ident[:], t_nodes[:, t:t + 1], None,
                                            ALU.mult).then_inc(la, 1)
                            if t >= 1:
                                v.wait_ge(lp, t)
                                v.tensor_copy(t_row[:, (t - 1) * P:t * P], tp[(t - 1) % 2][:, 0:P]).then_inc(wa_here, 1)
                        v.wait_ge(lp, TILES)
                        v.tensor_copy(t_row[:, (TILES - 1) * P:], tp[(TILES - 1) % 2][:, 0:P]).then_inc(wa_here, 1)

                @block.scalar
                def _(a):
                    n = TILES + 7
                    a.wait_ge(lv, n + 1)
                    a.activation(rstd[:], rec[:], ACT.Sqrt).then_inc(la, 1)
                    if layer == 1:
                        a.wait_ge(lv, n + 7)
                        a.activation(dinv[:], rec[:], ACT.Sqrt).then_inc(la, 1)

                if layer == 0:
                    @block.tensor
                    def _(pe):
                        for t in range(TILES):
                            pe.wait_ge(la, 2 + t)
                            if t >= 2:
                                pe.wait_ge(wa_here, 2 + t - 1)
                            pe.matmul(tp[t % 2][:, 0:P], ones[:], diag[:, t % 2, :],
                                      start=True, stop=True).then_inc(lp, 1)

        layer_norm(0)

        a_here = [sem(f"a_here{p}") for p in range(2)]
        a_free = [sem(f"a_free{p}") for p in range(2)]
        vq = sem("vq")
        expd = sem("expd")
        tpd = sem("tpd")
        tpc = sem("tpc")
        ypd = sem("ypd")
        epd = sem("epd")
        epc = sem("epc")
        opd = sem("opd")
        elu = sem("elu")
        NG = len(GROUPS)
        VT = 17
        with nc.Block() as block:
            @block.sync
            def _(sp):
                with sp.Fori(0, PAIRS) as k:
                    for p in range(2):
                        t = 2 * k + p
                        sp.wait_ge(a_free[p], k + 1)
                        sp.dma_start(abuf[:, p, :], adj[bass.ds(t * P, P), :]).then_inc(a_here[p], 16)

            @block.vector
            def _(v):
                for p in range(2):
                    v.nop().then_inc(a_free[p], 1)
                with v.Fori(0, PAIRS) as k:
                    for p in range(2):
                        t = 2 * k + p
                        base = t * VT
                        ab = abuf[:, p, :]

                        def step(inst, n):
                            inst.then_inc(vq, 1)
                            v.wait_ge(vq, base + n)
                        v.wait_ge(a_here[p], 16 * k + 16)
                        v.tensor_reduce(rowsum[:, bass.ds(t, 1)], ab, AX.X, ALU.add).then_inc(vq, 1)
                        step(v.tensor_scalar(ebuf[:], t_row[:], s_col[:, bass.ds(t, 1)], None, ALU.add), 2)
                        step(v.tensor_scalar(ab, ab, 0.0, None, ALU.is_gt), 3)
                        step(v.scalar_tensor_tensor(ebuf[:], ebuf[:], ALPHA, ebuf[:], ALU.mult, ALU.max), 4)
                        step(v.tensor_tensor(ebuf[:], ebuf[:], ab, ALU.mult), 5)
                        step(v.tensor_scalar(ab, ab, 1.0, MASKED, ALU.subtract, ALU.mult), 6)
                        v.wait_ge(tpd, 1 + 2 * NG * t)
                        step(v.tensor_tensor(prob[:, 0:N], ebuf[:, 0:N], ab[:, 0:N], ALU.add), 7)
                        v.tensor_reduce(nmax[:, 0:1], prob[:, 0:N], AX.X, ALU.max, negate=True).then_inc(vq, 1)
                        v.wait_ge(tpd, 1 + 2 * NG * t + NG)
                        step(v.scalar_tensor_tensor(prob[:, 0:N], ebuf[:, 0:N], -1.0, ab[:, 0:N], ALU.mult, ALU.add), 9)
                        v.tensor_reduce(nmax[:, 1:2], prob[:, 0:N], AX.X, ALU.max, negate=True).then_inc(a_free[p], 1)
                        v.wait_ge(expd, 2 * t + 2)
                        step(v.reciprocal(prec[:], psums[:]), 10)
                        step(v.tensor_scalar(prec[:, 1:2], prec[:, 1:2], -1.0, None, ALU.mult), 11)
                        v.wait_ge(ypd, 1 + 2 * t + 2)
                        for s in range(2):
                            v.tensor_scalar(y_sb[:, s * F:(s + 1) * F], yp[s][:, 0:F], prec[:, s:s + 1], None,
                                            ALU.mult).then_inc(vq, 1)
                        v.wait_ge(opd, t + 1)
                        v.tensor_scalar(elu_m[:], op[0][:, 0:F], 0.0, None, ALU.min).then_inc(vq, 1)
                        v.wait_ge(elu, t + 1)
                        v.tensor_scalar(elu_e[:], elu_e[:], -1.0, None, ALU.add).then_inc(vq, 1)
                        v.wait_ge(vq, base + 15)
                        v.scalar_tensor_tensor(elu_e[:], op[0][:, 0:F], 0.0, elu_e[:], ALU.max, ALU.add).then_inc(vq, 1)
                        v.wait_ge(vq, base + 16)
                        xt = xs[:, bass.ds(t, 1), :].rearrange("p a f -> p (a f)")
                        v.tensor_tensor(xt, xt, elu_e[:], ALU.add).then_inc(vq, 1)

            @block.scalar
            def _(a):
                with a.Fori(0, PAIRS) as k:
                    for p in range(2):
                        t = 2 * k + p
                        for s in range(2):
                            if s == 0:
                                a.wait_ge(vq, VT * t + 8)
                            else:
                                a.wait_ge(a_free[p], k + 2)
                            a.activation(prob[:, 0:N], prob[:, 0:N], ACT.Exp, bias=nmax[:, s:s + 1],
                                         accum_out=psums[:, s:s + 1]).then_inc(expd, 1)
                            for g, (j, n) in enumerate(GROUPS):
                                a.wait_ge(tpd, 1 + (2 * t + s) * NG + g + 1)
                                if g == 0:
                                    a.wait_ge(ypd, 1 + 2 * t + s)
                                a.activation(prob_t[:, j:j + n, :], tp[(s * NG + g) % 2][:, 0:n * P].rearrange("p (j i) -> p j i", j=n), ACT.Copy)\
                                 .then_inc(tpc, 1)
                        a.wait_ge(epd, t + 1)
                        a.activation(yt_sb[:], ep[0][:], ACT.Copy).then_inc(epc, 1)
                        a.wait_ge(vq, VT * t + 14)
                        a.activation(elu_e[:], elu_m[:], ACT.Exp).then_inc(elu, 1)

            @block.tensor
            def _(pe):
                pe.nop().then_inc(tpd, 1)
                pe.nop().then_inc(ypd, 1)
                with pe.Fori(0, PAIRS) as k:
                    for p in range(2):
                        t = 2 * k + p
                        for s in range(2):
                            pe.wait_ge(expd, 2 * t + s + 1)
                            for g, (j, n) in enumerate(GROUPS):
                                q = (2 * p + s) * NG + g
                                if q >= 2:
                                    pe.wait_ge(tpc, 4 * NG * k + q - 1)
                                for i in range(n):
                                    tr = pe.transpose(tp[(s * NG + g) % 2][:, i * P:(i + 1) * P],
                                                      prob[:, (j + i) * P:(j + i + 1) * P], ident[:])
                                tr.then_inc(tpd, 1)
                            pe.wait_ge(tpc, (2 * t + s + 1) * NG)
                            for j in range(TILES):
                                mm = pe.matmul(yp[s][:, 0:F], prob_t[:, j, :], h[:, j, :],
                                               start=(j == 0), stop=(j == TILES - 1))
                            mm.then_inc(ypd, 1)
                        pe.wait_ge(vq, VT * t + 13)
                        for c in range(2 * FB):
                            tr = pe.transpose(ep[0][:, c * P:(c + 1) * P], y_sb[:, c * P:(c + 1) * P], ident[:])
                        tr.then_inc(epd, 1)
                        pe.wait_ge(epc, t + 1)
                        for c in range(2 * FB):
                            mm = pe.matmul(op[0][:, 0:F], yt_sb[:, c * P:(c + 1) * P], wtrans_sb[:, c, :],
                                           start=(c == 0), stop=(c == 2 * FB - 1))
                        mm.then_inc(opd, 1)

        def graph_layer(layer):
            b_here = [sem(f"b_here{layer}_{p}") for p in range(2)]
            y_done = [sem(f"y_done{layer}_{p}") for p in range(2)]
            y_here = [sem(f"y_here{layer}_{p}") for p in range(2)]
            z_done = sem(f"z_done{layer}")
            zt_done = sem(f"zt_done{layer}")
            zt_here = sem(f"zt_here{layer}")
            o_done = sem(f"o_done{layer}")
            v_done = sem(f"v_done{layer}")
            with nc.Block() as block:
                @block.sync
                def _(sp):
                    with sp.Fori(0, PAIRS) as k:
                        for p in range(2):
                            t = 2 * k + p
                            sp.wait_ge(y_done[p], k + 1)
                            sp.dma_start(abuf[:, p, :], adj_t[bass.ds(t * P, P), :]).then_inc(b_here[p], 16)

                @block.tensor
                def _(pe):
                    for p in range(2):
                        pe.nop().then_inc(y_done[p], 1)
                    with pe.Fori(0, PAIRS) as k:
                        for p in range(2):
                            t = 2 * k + p
                            pe.wait_ge(b_here[p], 16 * k + 16)
                            pe.wait_ge(y_here[p], k + 1)
                            for j in range(TILES):
                                mm = pe.matmul(yp[p][:, 0:F], abuf[:, p, j * P:(j + 1) * P], h[:, j, :],
                                               start=(j == 0), stop=(j == TILES - 1))
                            mm.then_inc(y_done[p], 1)
                            pe.wait_ge(z_done, t + 1)
                            for c in range(FB):
                                tr = pe.transpose(ep[p][:, c * P:(c + 1) * P], y_sb[:, p * F + c * P:p * F + (c + 1) * P], ident[:])
                            tr.then_inc(zt_done, 1)
                            pe.wait_ge(zt_here, t + 1)
                            for c in range(FB):
                                mm = pe.matmul(op[p][:, 0:F], yt_sb[:, p * F + c * P:p * F + (c + 1) * P], w_sb[layer][:, c, :],
                                               start=(c == 0), stop=(c == FB - 1))
                            mm.then_inc(o_done, 1)

                @block.scalar
                def _(a):
                    with a.Fori(0, PAIRS) as k:
                        for p in range(2):
                            t = 2 * k + p
                            a.wait_ge(zt_done, t + 1)
                            a.activation(yt_sb[:, p * F:(p + 1) * F], ep[p][:, 0:F], ACT.Copy).then_inc(zt_here, 1)

                @block.vector
                def _(v):
                    for p in range(2):
                        v.nop().then_inc(y_here[p], 1)
                    with v.Fori(0, PAIRS) as k:
                        for p in range(2):
                            t = 2 * k + p
                            y, z = yp[p][:, 0:F], y_sb[:, p * F:(p + 1) * F]
                            xt = xs[:, bass.ds(t, 1), :].rearrange("p a f -> p (a f)")
                            ht = h[:, bass.ds(t, 1), :].rearrange("p a f -> p (a f)")
                            v.wait_ge(y_done[p], k + 2)
                            if layer == 1:
                                v.tensor_scalar(z, y, dinv[:, bass.ds(t, 1)], None, ALU.mult).then_inc(z_done, 1)
                                v.nop().then_inc(y_here[p], 1)
                            elif layer == 2:
                                v.tensor_copy(z, y).then_inc(z_done, 1)
                                v.nop().then_inc(y_here[p], 1)
                            else:
                                v.tensor_scalar(elu_m[:], y, t_col[:], None, ALU.mult).then_inc(y_here[p], 1)
                                v.wait_ge(y_here[p], k + 2)
                                v.scalar_tensor_tensor(z, ht, omt_col[:], elu_m[:], ALU.mult, ALU.add).then_inc(z_done, 1)
                            v.wait_ge(o_done, t + 1)
                            if layer == 1:
                                v.tensor_tensor(elu_e[:], op[p][:, 0:F], b_row[:], ALU.add).then_inc(v_done, 1)
                                v.wait_ge(v_done, 2 * t + 1)
                                v.scalar_tensor_tensor(xt, elu_e[:], 0.0, xt, ALU.max, ALU.add).then_inc(v_done, 1)
                            elif layer == 2:
                                v.scalar_tensor_tensor(xt, op[p][:, 0:F], 0.0, xt, ALU.max, ALU.add).then_inc(v_done, 1)
                            else:
                                v.tensor_tensor(xt, op[p][:, 0:F], xt, ALU.add).then_inc(v_done, 1)

        for layer in (1, 2, 3):
            layer_norm(layer)
            graph_layer(layer)

        stored = sem("stored")
        with nc.Block() as block:
            @block.sync
            def _(sp):
                full = (TILES - 1) * P
                sp.dma_start(out[0:full, :].rearrange("(t p) f -> p t f", p=P), xs[:, 0:TILES - 1, :]).then_inc(stored, 16)
                sp.dma_start(out[full:N, :], xs[0:N - full, TILES - 1, :]).then_inc(stored, 16)
                sp.wait_ge(stored, 32)


def fast_program(nc, io, general, prefix="f_"):
    with ExitStack() as ctx:
        def sb(name, shape, dt=F32):
            return ctx.enter_context(nc.sbuf_tensor(prefix + name, shape, dt))

        def sem(name):
            return ctx.enter_context(nc.semaphore(prefix + name))

        HALF = TILES // 2
        HW = HALF * P

        xs = sb("xs", [P, TILES, F])
        ident = sb("ident", [P, P])
        ones = sb("ones", [P, P])
        w_att_sb = sb("w_att_sb", [P, FB, F])
        a_sb = sb("a_sb", [P, 2, FB])
        wtrans_sb = sb("wtrans_sb", [P, 2 * FB, F])
        w_sb = {l: sb(f"w{l}_sb", [P, FB, F]) for l in (1, 2, 3)}
        b_row = sb("b_row", [P, F])
        t_col = sb("t_col", [P, 1])
        t_scaled = sb("t_scaled", [P, 1])
        omt_scaled = sb("omt_scaled", [P, 1])
        wa = sb("wa", [P, 2, F])
        xh = {(g, part): sb(f"x{g}_{part}", [P, TILES, 2 * F], F16) for g in range(2) for part in range(2)}
        x_layer = {1: xh[0, 0], 2: xh[0, 1], 3: xh[1, 0]}
        dcol = sb("dcol", [P, TILES, 2, 5], F16)
        adj32 = sb("adj32", [P, 2, HW])
        a8 = sb("a8", [P, 2, NP], F8)
        a8_pair = adj32[:].rearrange("p r c -> p (r c)").bitcast(F8).rearrange("p (r w c) -> p r w c", r=2, w=2)
        above = sb("above", [P, 2, NP], F8)
        below = sb("below", [P, 2, NP], F8)
        score = sb("score", [P, HW])
        s_tile = sb("s_tile", [P, 2, P])
        s_col = sb("s_col", [P, TILES])
        t_nodes = sb("t_nodes", [P, TILES])
        s_rows = sb("s_rows", [TILES, P])
        ext = sb("ext", [P, 2])
        ext_neg = sb("ext_neg", [P, 4])
        colf = sb("colf", [P, 2, 2, TILES])
        colx = sb("colx", [P, 2, 2, TILES])
        fac = sb("fac", [P, TILES, 4])
        farg = sb("farg", [P, 4, TILES])
        stats = sb("stats", [P, TILES, 6])
        mean = sb("mean", [P, TILES])
        var = sb("var", [P, TILES])
        rec = sb("rec", [P, TILES])
        rstd = sb("rstd", [P, TILES])
        rowsum = sb("rowsum", [P, TILES])
        dinv = sb("dinv", [P, TILES])
        minus_half = sb("minus_half", [P, TILES])
        bad = sb("bad", [P, 2 * TILES])
        flags = sb("flags", [P, 4])
        ubuf = sb("ubuf", [P, 2, F])
        csb = sb("csb", [P, 2, 5])
        dsum = sb("dsum", [P, 4])
        den = sb("den", [P, 2])
        rfac = sb("rfac", [P, 2, 4])
        tb = sb("tb", [P, 2 * F])
        y_sb = sb("y_sb", [P, 2, 2 * F])
        yt_sb = sb("yt_sb", [P, 2 * F])
        ex = sb("ex", [P, F])
        w_res = sb("w_res", [P, F])
        mv = sb("mv", [P, 2, 2])
        cst = sb("cst", [P, 2])
        xo = sb("xo", [P, 2, F])
        gv = sb("gv", [P, 2])
        gm = sb("gm", [P, 1])
        stl = sb("stl", [P, 2, 6])

        def ps(name):
            return ctx.enter_context(nc.psum_tensor(prefix + name, [P, 512], F32))
        bank_a = [ps(f"bank_a{p}") for p in range(2)]
        bank_b = [ps(f"bank_b{p}") for p in range(2)]
        bank_c = [ps(f"bank_c{p}") for p in range(2)]
        ep, op = ps("ep"), ps("op")

        a8_dram = nc.dram_tensor(prefix + "a8_dram", (TILES, P, NP), U8).ap()
        s_dram = nc.dram_tensor(prefix + "s_dram", (TILES, P), F32).ap()
        adj_t = io["adj_t"]

        always = sem("always")
        waited = sem("waited")
        x_here = [sem(f"x_here{c}") for c in range(4)]
        w_here = sem("w_here")
        late_here = sem("late_here")
        prep = sem("prep")
        ln = sem("ln")
        powd = sem("powd")
        wa_done = sem("wa_done")
        dotd = sem("dotd")
        st_done = sem("st_done")
        s_stored = sem("s_stored")
        extd = sem("extd")
        expd = sem("expd")
        xlo = sem("xlo")
        xhi = sem("xhi")
        ud = sem("ud")
        adj_here = [sem(f"adj_here{i}") for i in range(2)]
        s_here = [sem(f"s_here{i}") for i in range(2)]
        cast_done = sem("cast_done")
        check_done = sem("check_done")
        a8_stored = [sem(f"a8_stored{i}") for i in range(2)]
        score_done = sem("score_done")
        masks_done = sem("masks_done")
        main_done = sem("main_done")
        small = sem("small")
        tb_done = sem("tb_done")
        y_done = sem("y_done")
        yt_psum = sem("yt_psum")
        yt_done = sem("yt_done")
        o_done = sem("o_done")
        ex_done = sem("ex_done")
        x_done = sem("x_done")
        xc = sem("xc")
        L = (1, 2, 3)
        pair_here = {(l, r): sem(f"pair_here{l}{r}") for l in L for r in range(2)}
        mm_done = {l: sem(f"mm_done{l}") for l in L}
        tl_done = {l: sem(f"tl_done{l}") for l in L}
        zc = {l: sem(f"zc{l}") for l in L}
        z_done = {l: sem(f"z_done{l}") for l in L}
        zt_psum = {l: sem(f"zt_psum{l}") for l in L}
        zt_done = {l: sem(f"zt_done{l}") for l in L}
        p_done = {l: sem(f"p_done{l}") for l in L}
        upd = {l: sem(f"upd{l}") for l in L}
        read_o = {l: sem(f"read_o{l}") for l in L}
        uhi = sem("uhi")
        x_ready = {l: sem(f"x_ready{l}") for l in L}
        aggd = sem("aggd")
        nrm = sem("nrm")
        rstdd = sem("rstdd")
        stored = [sem(f"stored{p}") for p in range(2)]
        flagd = sem("flagd")
        flc = sem("flc")
        vp = sem("vp")
        dots = sem("dots")
        xhp = sem("xhp")
        wready = sem("wready")
        gs = sem("gs")

        XCH = [(0, 7), (7, 14), (14, 20), (20, 26)]
        LN_STEPS = 7
        A_STEPS = 7

        def in_pairs(eng, pair):
            pair(0, True)
            with eng.Fori(1, PAIRS) as k:
                pair(k, False)

        with nc.Block() as block:
            @block.sync
            def _(sp):
                def wait(signal, value):
                    sp.wait_ge(signal, value)
                    if not isinstance(value, int):
                        sp.sem_inc(waited, 1)

                for c, (j0, j1) in enumerate(XCH):
                    sp.dma_start(xs[:, j0:j1, :], io["x"][:, j0:j1, :]).then_inc(x_here[c], 16)

                def load_half(t, hf):
                    sp.dma_start(adj32[:, hf, :], adj_t[bass.ds(t * P, P), hf * HW:(hf + 1) * HW])\
                      .then_inc(adj_here[hf], 16)

                def load_s(t, p):
                    sp.dma_start(s_tile[:, p, :], s_dram[bass.ds(t, 1), :].broadcast_to([P, P])).then_inc(s_here[p], 16)

                def pair(k, first):
                    for p in range(2):
                        t = 2 * k + p
                        for hf in range(2):
                            if not (first and p == 0):
                                wait(cast_done, 2 * t + hf - 1)
                                wait(check_done, 2 * t + hf - 1)
                            load_half(t, hf)
                        if first and p == 0:
                            wait(st_done, 2)
                            sp.dma_start(s_dram, s_rows[:]).then_inc(s_stored, 16)
                            wait(s_stored, 16)
                        if not first:
                            wait(score_done, 2 * t - 2)
                        load_s(t, p)
                        if not (first and p == 0):
                            wait(cast_done, 2 * t)
                            sp.dma_start(a8_dram[bass.ds(t - 1, 1), :, :].rearrange("a p c -> p (a c)"),
                                         a8[:, 1 - p, :].bitcast(U8)).then_inc(a8_stored[1 - p], 16)
                in_pairs(sp, pair)
                wait(cast_done, 2 * TILES)
                sp.dma_start(a8_dram[TILES - 1], a8[:, 1, :].bitcast(U8)).then_inc(a8_stored[1], 16)

                wait(check_done, 2 * TILES)
                for p in range(2):
                    wait(a8_stored[p], 16 * PAIRS)

                def load_pair(layer, q, r):
                    sp.dma_start(a8_pair[:, r].bitcast(U8),
                                 a8_dram[bass.ds(2 * q, 2), :, :].rearrange("w p c -> p w c"))\
                      .then_inc(pair_here[layer, r], 16)

                def store(q, last=False):
                    for p in range(2):
                        t = 2 * q + p
                        wait(upd[3], t + 1)
                        rows = N - (TILES - 1) * P if last and p else P
                        sp.dma_start(io["out"][bass.ds(t * P, rows), :], xo[0:rows, p, :]).then_inc(stored[p], 16)

                for layer in L:
                    def next_pair(q, r, load=True):
                        wait(mm_done[layer], 2 * q + 2)
                        load_pair(layer, q + 2, r)

                    r0 = layer % 2 ^ 1
                    if layer > 1:
                        wait(mm_done[layer - 1], TILES - 2)
                    load_pair(layer, 0, r0)
                    if layer > 1:
                        wait(mm_done[layer - 1], TILES)
                    load_pair(layer, 1, r0 ^ 1)
                    with sp.Fori(0, (PAIRS - 3) // 2) as k:
                        for i in range(2):
                            next_pair(2 * k + i, r0 ^ i)
                            if layer == 3:
                                store(2 * k + i)
                    next_pair(PAIRS - 3, r0)
                    if layer == 3:
                        for q in range(PAIRS - 3, PAIRS):
                            store(q, q == PAIRS - 1)
                for p in range(2):
                    wait(stored[p], 16 * PAIRS)

            @block.gpsimd
            def _(g):
                g.memset(minus_half[:], -0.5).then_inc(always, 1)
                g.wait_ge(always, 1)

                def inverse_root(o, i, waited):
                    g.wait_ge(ln, waited)
                    g.tensor_tensor(o, i, minus_half[:], ALU.pow).then_inc(powd, 1)
                inverse_root(rstd[:], var[:], LN_STEPS)

                def x0_block(j, p):
                    g.wait_ge(ud, j + 1)
                    g.sem_inc(waited, 1)
                    g.tensor_tensor(xh[1, 0][:, bass.ds(j, 1), F:2 * F], ubuf[:, p:p + 1, :],
                                    colx[:, 1, 1:2, bass.ds(j, 1)].broadcast_to([P, 1, F]), ALU.mult).then_inc(xhp, 1)
                with g.Fori(0, PAIRS) as k:
                    for p in range(2):
                        x0_block(2 * k + p, p)
                inverse_root(rstd[:], var[:], 2 * LN_STEPS)
                inverse_root(dinv[:], rec[:], 2 * LN_STEPS + 1)

                with g.Fori(0, PAIRS) as k:
                    for p in range(2):
                        t = 2 * k + p
                        g.wait_ge(aggd, t + 1)
                        g.sem_inc(waited, 1)
                        g.tensor_scalar(gv[:, p:p + 1], mv[:, p, 1:2], EPS, None, ALU.add).then_inc(gs, 1)
                        g.wait_ge(gs, 2 * t + 1)
                        g.sem_inc(waited, 1)
                        g.tensor_tensor(gv[:, p:p + 1], gv[:, p:p + 1], minus_half[:, 0:1], ALU.pow).then_inc(gs, 1)
                        g.wait_ge(gs, 2 * t + 2)
                        g.sem_inc(waited, 1)
                        g.tensor_scalar(cst[:, p:p + 1], gv[:, p:p + 1], SCALE, None, ALU.mult).then_inc(rstdd, 1)

            @block.scalar
            def _(a):
                def settle():
                    a.sem_inc(waited, 1)
                a.dma_start(w_att_sb[:], io["w_att_t"].rearrange("(c p) f -> p c f", p=P)).then_inc(w_here, 16)
                a.dma_start(a_sb[:], io["a_vec"].rearrange("p (s c) -> p s c", s=2)).then_inc(w_here, 16)
                a.dma_start(ident[:], io["ident"]).then_inc(w_here, 16)
                a.dma_start(wtrans_sb[:], io["wtrans"].rearrange("(c p) f -> p c f", p=P)).then_inc(late_here, 16)
                for layer, w in ((1, "w1"), (2, "w2_t"), (3, "w3")):
                    a.dma_start(w_sb[layer][:], io[w].rearrange("(c p) f -> p c f", p=P)).then_inc(late_here, 16)
                a.dma_start(b_row[:], io["b1"].rearrange("(a f) -> a f", a=1).broadcast_to([P, F])).then_inc(late_here, 16)
                a.dma_start(t_col[:], io["t3"].rearrange("(a f) -> a f", a=1).broadcast_to([P, 1])).then_inc(late_here, 16)

                def cast(t, p, pair_k, first):
                    for hf in range(2):
                        a.wait_ge(adj_here[hf], 16 * t + 16)
                        if hf == 0 and not first:
                            a.wait_ge(a8_stored[p], 16 * pair_k)
                            a.wait_ge(masks_done, 4 * t - 4)
                        settle()
                        a.activation(a8[:, p, hf * HW:(hf + 1) * HW], adj32[:, hf, :], ACT.Copy, saturate=False).then_inc(cast_done, 1)

                a.wait_ge(st_done, 1)
                a.activation(s_rows[:], ep[0:TILES, 0:P], ACT.Copy).then_inc(st_done, 1)
                cast(0, 0, 0, True)
                a.wait_ge(extd, 2)
                a.activation(colf[:], colx[:], ACT.Exp).then_inc(expd, 1)
                a.wait_ge(extd, 3)
                a.activation(fac[:].rearrange("p t g -> p g t"), farg[:], ACT.Exp).then_inc(expd, 1)

                def x0_block(j, p):
                    a.wait_ge(ud, j + 1)
                    for g, s in ((0, 0), (0, 1), (1, 0)):
                        a.activation(xh[g, 0][:, bass.ds(j, 1), s * F:(s + 1) * F], ubuf[:, p:p + 1, :], ACT.Copy,
                                     scale=colx[:, g, s, bass.ds(j, 1)]).then_inc(xhi, 1)
                with a.Fori(0, PAIRS) as k:
                    for p in range(2):
                        x0_block(2 * k + p, p)

                def turn_copy(t):
                    a.wait_ge(yt_psum, t + 1)
                    a.activation(yt_sb[:], ep[:], ACT.Copy).then_inc(yt_done, 1)

                def elu_exp(t, first=False):
                    a.wait_ge(o_done, t + 1)
                    if not first:
                        a.wait_ge(x_done, t)
                    a.activation(ex[:], op[:, 0:F], ACT.Exp).then_inc(ex_done, 1)

                def below_part(t, p):
                    a.wait_ge(small, A_STEPS * t + A_STEPS)
                    for s in range(2):
                        a.activation(tb[:, s * F:(s + 1) * F], bank_b[p][:, s * F:(s + 1) * F], ACT.Copy,
                                     scale=rfac[:, p, 2 + s:3 + s]).then_inc(tb_done, 1)

                def pair(k, first):
                    for p in range(2):
                        t = 2 * k + p
                        if not (first and p == 0):
                            cast(t, p, k, first)
                        if not first:
                            turn_copy(t - 2)
                            elu_exp(t - 2, False)
                        if not (first and p == 0):
                            below_part(t - 1, 1 - p)
                pair(0, True)
                with a.Fori(1, PAIRS) as k:
                    pair(k, False)
                turn_copy(TILES - 2)
                elu_exp(TILES - 2)
                below_part(TILES - 1, 1)
                turn_copy(TILES - 1)
                elu_exp(TILES - 1)

                def x1_block(j, p):
                    a.wait_ge(ud, TILES + j + 1)
                    a.activation(x_layer[1][:, bass.ds(j, 1), 0:F], ubuf[:, p:p + 1, :], ACT.Copy,
                                 scale=colx[:, 0, 0, bass.ds(j, 1)]).then_inc(xhi, 1)
                with a.Fori(0, PAIRS) as k:
                    for p in range(2):
                        x1_block(2 * k + p, p)

                for layer in L:
                    def product(t, p):
                        a.wait_ge(mm_done[layer], t + 1)
                        if layer == 2:
                            a.activation(y_sb[:, p, 0:F], bank_a[p][:, 0:F], ACT.Copy).then_inc(z_done[2], 1)
                        else:
                            scale = dinv[:, bass.ds(t, 1)] if layer == 1 else t_scaled[:]
                            a.activation(tb[:, p * F:(p + 1) * F], bank_a[p][:, F:2 * F], ACT.Copy,
                                         scale=scale).then_inc(tl_done[layer], 1)

                    def turned(t):
                        a.wait_ge(zt_psum[layer], t + 1)
                        a.activation(yt_sb[:, 0:F], ep[:, 0:F], ACT.Copy).then_inc(zt_done[layer], 1)

                    def pair(k, first):
                        for p in range(2):
                            t = 2 * k + p
                            if not (first and p == 0):
                                turned(t - 1)
                            product(t, p)
                    in_pairs(a, pair)
                    turned(TILES - 1)

            @block.tensor
            def _(pe):
                def settle():
                    pe.sem_inc(waited, 1)
                pe.wait_ge(prep, 4)
                rep = score[:, 0:2 * FB * P].rearrange("p (s c m) -> p s c m", s=2, c=FB)
                for s in range(2):
                    for c in range(FB):
                        mm = pe.matmul(op[:, s * F:(s + 1) * F], rep[:, s, c, :], w_att_sb[:, c, :],
                                       start=(c == 0), stop=(c == FB - 1))
                mm.then_inc(wa_done, 1)
                pe.wait_ge(dotd, 1)
                pe.transpose(ep[0:TILES, 0:P], s_col[:], ident[:]).then_inc(st_done, 1)
                pe.wait_ge(dotd, 6)
                pe.matmul(op[:, 0:2 * P], ones[:], y_sb[:, 0, 0:2 * P], start=True, stop=True).then_inc(extd, 1)

                def turn(t, p, done, ready, blocks, per=1):
                    pe.wait_ge(ready, per * t + per)
                    for c in range(blocks):
                        tr = pe.transpose(ep[:, c * P:(c + 1) * P], y_sb[:, p, c * P:(c + 1) * P], ident[:])
                    tr.then_inc(done, 1)

                def project(t, w, blocks, turned, done):
                    pe.wait_ge(turned, t + 1)
                    for c in range(blocks):
                        mm = pe.matmul(op[:, 0:F], yt_sb[:, c * P:(c + 1) * P], w[:, c, :],
                                       start=(c == 0), stop=(c == blocks - 1))
                    mm.then_inc(done, 1)

                def attention_epilogue(t, p, part, first=False):
                    if part == 0:
                        turn(t, p, yt_psum, y_done, 2 * FB, 2)
                    else:
                        if first:
                            pe.wait_ge(late_here, 16 * 6)
                        else:
                            pe.wait_ge(xc, 3 * t - 1)
                            pe.wait_ge(ex_done, t)
                        project(t, wtrans_sb, 2 * FB, yt_done, o_done)

                def main(t, p, k, first):
                    for j in range(TILES):
                        if j % HALF == 0:
                            pe.wait_ge(masks_done, 4 * t + 2 * (j // HALF) + 2)
                            if j == 0 and not first:
                                pe.wait_ge(y_done, 2 * t - 2)
                            settle()
                        if first and p == 0:
                            pe.wait_ge(xlo, 4 * j + 4)
                        if not (first and p == 0) and j in (8, 14):
                            attention_epilogue(t - 1, 1 - p, (8, 14).index(j), first and p == 1)
                        lo, hi = j * P, (j + 1) * P
                        for g, (mask, bank) in enumerate(((above, bank_a[p]), (below, bank_b[p]))):
                            pe.matmul(bank[:], mask[:, p, lo:hi], xh[g, 0][:, j, :], start=(j == 0), stop=False)
                            pe.matmul(bank[:], mask[:, p, lo:hi], xh[g, 1][:, j, :], start=False, stop=(j == TILES - 1))
                            mm = pe.matmul(bank_c[p][:, 5 * g:5 * g + 5], mask[:, p, lo:hi], dcol[:, j, g, :],
                                           start=(j == 0 and g == 0), stop=(j == TILES - 1), skip_group_check=True)
                    mm.then_inc(main_done, 1)

                def pair(k, first):
                    for p in range(2):
                        main(2 * k + p, p, k, first)
                in_pairs(pe, pair)
                attention_epilogue(TILES - 1, 1, 0)
                attention_epilogue(TILES - 1, 1, 1)

                for layer in L:
                    W = F if layer == 2 else 2 * F
                    r0 = layer % 2 ^ 1

                    def epilogue(t, p, part, first=False):
                        if part == 0:
                            turn(t, p, zt_psum[layer], z_done[layer], FB)
                        else:
                            if first and layer == 1:
                                pe.wait_ge(x_done, TILES)
                            elif first:
                                pe.wait_ge(read_o[layer - 1], TILES)
                            else:
                                pe.wait_ge(read_o[layer], t)
                            project(t, w_sb[layer], FB, zt_done[layer], p_done[layer])

                    def tile(q, p, r, n, first):
                        t = 2 * q + p
                        if first and p == 0:
                            pe.wait_ge(pair_here[layer, r], 16)
                        elif p == 0:
                            pe.wait_ge(pair_here[layer, r], n)
                        if not first:
                            pe.wait_ge(z_done[layer], t - 1)
                        elif layer == 1:
                            pe.wait_ge(y_done, 2 * TILES)
                        else:
                            pe.wait_ge(z_done[layer - 1], TILES - 1 + p)
                        settle()
                        for j in range(TILES):
                            if first and p == 0:
                                pe.wait_ge(x_ready[layer], j + 1)
                            if not (first and p == 0) and j in (10, 20):
                                epilogue(t - 1, 1 - p, (10, 20).index(j), first)
                            mm = pe.matmul(bank_a[p][:, 0:W], a8_pair[:, r, p, j * P:(j + 1) * P], x_layer[layer][:, j, 0:W],
                                           start=(j == 0), stop=(j == TILES - 1))
                        mm.then_inc(mm_done[layer], 1)
                    for p in range(2):
                        tile(0, p, r0, 16, True)
                    with pe.Fori(0, PAIRS // 2) as k:
                        for i in range(2):
                            q = 2 * k + 1 + i
                            for p in range(2):
                                tile(q, p, r0 ^ 1 ^ i, 16 * k + 16 + 16 * i, False)
                    epilogue(TILES - 1, 1, 0)
                    epilogue(TILES - 1, 1, 1)
                    if layer == 1:
                        pe.wait_ge(flagd, 1)
                        pe.matmul(bank_c[0][:, 0:1], ones[:], flags[:, 3:4], start=True, stop=True).then_inc(flagd, 1)

            @block.vector
            def _(v):
                def settle():
                    v.sem_inc(waited, 1)
                v.memset(ones[:], 1.0).then_inc(vp, 1)
                v.memset(dcol[:], 1.0).then_inc(vp, 1)
                v.wait_ge(w_here, 48)
                v.wait_ge(vp, 2)
                rep = score[:, 0:2 * FB * P].rearrange("p (s c m) -> p s c m", s=2, c=FB)
                for s in range(2):
                    for c in range(FB):
                        v.tensor_scalar(rep[:, s, c, :], ones[:], a_sb[:, s, c:c + 1], None, ALU.mult).then_inc(prep, 1)
                for c, (j0, j1) in enumerate(XCH):
                    v.wait_ge(x_here[c], 16)
                    for j in range(j0, j1):
                        v.bn_stats(stats[:, j, :], xs[:, j, :]).then_inc(vp, 1)
                v.wait_ge(wa_done, 1)
                v.tensor_copy(wa[:], op[:].rearrange("p (s f) -> p s f", s=2)).then_inc(vp, 1)
                v.wait_ge(vp, 2 + TILES + 1)

                def chain(sem, n):
                    count = [n]

                    def step(inst):
                        inst.then_inc(sem, 1)
                        count[0] += 1
                        v.wait_ge(sem, count[0])
                    return step

                def row_stats(n):
                    step = chain(ln, n)
                    step(v.tensor_tensor(mean[:], stats[:, :, 1], stats[:, :, 4], ALU.add))
                    step(v.tensor_scalar(mean[:], mean[:], 0.5, None, ALU.mult))
                    step(v.tensor_tensor(rec[:], stats[:, :, 1], stats[:, :, 4], ALU.subtract))
                    step(v.scalar_tensor_tensor(rec[:], rec[:], 0.25, rec[:], ALU.mult, ALU.mult))
                    step(v.tensor_tensor(var[:], stats[:, :, 2], stats[:, :, 5], ALU.add))
                    step(v.scalar_tensor_tensor(var[:], var[:], 1.0 / F, rec[:], ALU.mult, ALU.add))
                    step(v.tensor_scalar(var[:], var[:], EPS, None, ALU.add))
                row_stats(0)

                def centred(j, p, sem):
                    v.tensor_scalar(ubuf[:, p:p + 1, :], xs[:, bass.ds(j, 1), :], mean[:, bass.ds(j, 1)], 0.0,
                                    ALU.subtract, ALU.max).then_inc(sem, 1)

                with v.Fori(0, PAIRS) as k:
                    for p in range(2):
                        j = 2 * k + p
                        centred(j, p, dots)
                        v.wait_ge(dots, 3 * j + 1)
                        for s, o in enumerate((s_col, t_nodes)):
                            v.scalar_tensor_tensor(w_res[:] if s else ex[:], ubuf[:, p, :], 1.0, wa[:, s, :], ALU.mult, ALU.mult,
                                                   accum_out=o[:, bass.ds(j, 1)]).then_inc(dots, 1)
                v.wait_ge(dots, 3 * TILES)
                v.wait_ge(powd, 1)
                v.tensor_tensor(s_col[:], s_col[:], rstd[:], ALU.mult).then_inc(dotd, 1)
                step = chain(dotd, 1)
                step(v.tensor_tensor(t_nodes[:], t_nodes[:], rstd[:], ALU.mult))
                step(v.tensor_reduce(ext[:, 0:1], t_nodes[:], AX.X, ALU.max))
                step(v.tensor_reduce(ext[:, 1:2], t_nodes[:], AX.X, ALU.min))
                step(v.tensor_scalar(y_sb[:, 0, 0:P], ident[:], ext[:, 0:1], None, ALU.mult))
                step(v.tensor_scalar(y_sb[:, 0, P:2 * P], ident[:], ext[:, 1:2], None, ALU.mult))
                v.wait_ge(extd, 1)
                step(v.tensor_reduce(ext[:, 0:1], op[:, 0:P], AX.X, ALU.max))
                step(v.tensor_reduce(ext[:, 1:2], op[:, P:2 * P], AX.X, ALU.min))
                for g, rate in enumerate((1.0, ALPHA)):
                    step(v.tensor_scalar(colx[:, g, 0, :], t_nodes[:], ext[:, 0:1], rate, ALU.subtract, ALU.mult))
                    last = v.tensor_scalar(colx[:, g, 1, :], t_nodes[:], ext[:, 1:2], -rate, ALU.subtract, ALU.mult)
                    if g == 0:
                        step(last)
                last.then_inc(extd, 1)
                gap = 1.0 - ALPHA
                step(v.tensor_scalar(farg[:, 0, :], s_col[:], ext[:, 0:1], gap, ALU.add, ALU.mult))
                step(v.tensor_scalar(farg[:, 1, :], s_col[:], ext[:, 1:2], -gap, ALU.add, ALU.mult))
                step(v.tensor_scalar(farg[:, 2, :], farg[:, 0, :], -1.0, 0.0, ALU.mult, ALU.min))
                step(v.tensor_scalar(farg[:, 0, :], farg[:, 0, :], 0.0, None, ALU.min))
                step(v.tensor_scalar(farg[:, 3, :], farg[:, 1, :], -1.0, 0.0, ALU.mult, ALU.max))
                step(v.tensor_scalar(farg[:, 1, :], farg[:, 1, :], 0.0, SPREAD - 1.0, ALU.max, ALU.min))
                v.tensor_scalar(farg[:, 3, :], farg[:, 3, :], SPREAD - 1.0, None, ALU.min).then_inc(extd, 1)
                v.wait_ge(expd, 2)
                step(v.tensor_scalar(colx[:], colf[:], SCALE, None, ALU.mult))
                cview = colx[:].rearrange("p g s t -> p t g s")
                step(v.tensor_copy(dcol[:, :, :, 0:2], cview))
                step(v.tensor_tensor(dcol[:, :, :, 2:4], cview, dcol[:, :, :, 0:2], ALU.subtract))
                step(v.tensor_tensor(colx[:].rearrange("p g s t -> p (g s) t"), colx[:].rearrange("p g s t -> p (g s) t"),
                                     rstd[:].rearrange("p (a t) -> p a t", a=1).broadcast_to([P, 4, TILES]), ALU.mult))

                def prepare(t, p, k, first):
                    for hf in range(2):
                        q = 2 * t + hf
                        v.wait_ge(adj_here[hf], 16 * t + 16)
                        if not (first and p == 0 and hf == 0):
                            v.wait_ge(masks_done, 2 * q)
                        a32 = adj32[:, hf, :]
                        v.scalar_tensor_tensor(score[:], a32, 0.0, a32, ALU.is_gt, ALU.not_equal,
                                               accum_out=bad[:, bass.ds(q, 1)]).then_inc(check_done, 1)
                        v.wait_ge(check_done, q + 1)
                        if hf == 0:
                            v.wait_ge(s_here[p], 16 * k + 16)
                        tj = t_nodes[:, hf * HALF:(hf + 1) * HALF].rearrange("p (j a) -> p j a", a=1).broadcast_to([P, HALF, P])
                        si = s_tile[:, p:p + 1, :].broadcast_to([P, HALF, P])
                        v.tensor_tensor(score[:].rearrange("p (j i) -> p j i", j=HALF), tj, si, ALU.add)\
                         .then_inc(score_done, 1)
                        v.wait_ge(score_done, q + 1)
                        v.wait_ge(cast_done, q + 1)
                        if hf == 0 and not first:
                            v.wait_ge(main_done, t - 1)
                        settle()
                        part = slice(hf * HW, (hf + 1) * HW)
                        v.scalar_tensor_tensor(above[:, p, part], score[:], 0.0, a8[:, p, part], ALU.is_gt, ALU.mult,
                                               saturate=False).then_inc(masks_done, 1)
                        v.scalar_tensor_tensor(below[:, p, part], score[:], 0.0, a8[:, p, part], ALU.is_le, ALU.mult,
                                               saturate=False).then_inc(masks_done, 1)

                prepare(0, 0, 0, True)

                def low_parts(j, p):
                    for n, (g, s) in enumerate(((0, 0), (0, 1), (1, 0), (1, 1))):
                        if n < 3:
                            v.wait_ge(xhi, 3 * j + n + 1)
                        else:
                            v.wait_ge(xhp, j + 1)
                        cols = slice(s * F, (s + 1) * F)
                        v.scalar_tensor_tensor(xh[g, 1][:, bass.ds(j, 1), cols], ubuf[:, p:p + 1, :],
                                               colx[:, g, s, bass.ds(j, 1)], xh[g, 0][:, bass.ds(j, 1), cols],
                                               ALU.mult, ALU.subtract).then_inc(xlo, 1)
                centred(0, 0, ud)
                centred(1, 1, ud)
                low_parts(0, 0)
                with v.Fori(1, PAIRS) as k:
                    for p in range(2):
                        j = 2 * k + p
                        v.wait_ge(xlo, 4 * j - 4)
                        centred(j, p, ud)
                        low_parts(j - 1, 1 - p)
                low_parts(TILES - 1, 1)

                v.wait_ge(late_here, 96)
                v.wait_ge(xlo, 4 * TILES)
                w2v = w_sb[2][:]
                scr = ubuf[:]
                step(v.tensor_scalar(scr, w2v, 0.0, None, ALU.is_gt))
                step(v.tensor_scalar(w2v, w2v, 0.0, None, ALU.is_lt))
                step(v.tensor_tensor(w2v, scr, w2v, ALU.subtract))
                step(v.tensor_scalar(wtrans_sb[:, FB:2 * FB, :], wtrans_sb[:, FB:2 * FB, :], -1.0, None, ALU.mult))
                step(v.tensor_scalar(t_scaled[:], t_col[:], 1.0 / SCALE, None, ALU.mult))
                v.tensor_scalar(omt_scaled[:], t_col[:], -1.0 / SCALE, 1.0 / SCALE, ALU.mult, ALU.add).then_inc(wready, 1)

                def combine(t, p):
                    n = A_STEPS * t
                    v.wait_ge(main_done, t + 1)
                    cs = csb[:]
                    v.tensor_copy(cs, bank_c[p][:, 0:10].rearrange("p (g c) -> p g c", g=2)).then_inc(small, 1)
                    v.wait_ge(small, n + 1)
                    v.tensor_tensor(dsum[:].rearrange("p (g s) -> p g s", g=2), csb[:, :, 0:2], csb[:, :, 2:4], ALU.add).then_inc(small, 1)
                    v.tensor_tensor(rowsum[:, bass.ds(t, 1)], csb[:, 0, 4:5], csb[:, 1, 4:5], ALU.add).then_inc(small, 1)
                    v.wait_ge(small, n + 2)
                    f = fac[:, bass.ds(t, 1), :].rearrange("p a g -> p (a g)")
                    v.tensor_tensor(dsum[:], dsum[:], f, ALU.mult).then_inc(small, 1)
                    v.wait_ge(small, n + 4)
                    v.scalar_tensor_tensor(den[:], dsum[:, 0:2], TINY, dsum[:, 2:4], ALU.max, ALU.add).then_inc(small, 1)
                    v.wait_ge(small, n + 5)
                    v.reciprocal(den[:], den[:]).then_inc(small, 1)
                    v.wait_ge(small, n + 6)
                    v.tensor_tensor(rfac[:, p, :].rearrange("p (g s) -> p g s", g=2), f.rearrange("p (g s) -> p g s", g=2),
                                    den[:].rearrange("p (a s) -> p a s", a=1).broadcast_to([P, 2, 2]), ALU.mult).then_inc(small, 1)
                    v.wait_ge(small, n + 7)
                    for s in range(2):
                        v.wait_ge(tb_done, 2 * t + s + 1)
                        cols = slice(s * F, (s + 1) * F)
                        v.scalar_tensor_tensor(y_sb[:, p, cols], bank_a[p][:, cols], rfac[:, p, s:s + 1], tb[:, cols],
                                               ALU.mult, ALU.add).then_inc(y_done, 1)

                def elu(t):
                    xt = xs[:, bass.ds(t, 1), :].rearrange("p a f -> p (a f)")
                    v.wait_ge(ex_done, t + 1)
                    v.scalar_tensor_tensor(w_res[:], op[:, 0:F], 0.0, xt, ALU.max, ALU.add).then_inc(xc, 1)
                    v.tensor_scalar(ex[:], ex[:], 1.0, -1.0, ALU.min, ALU.add).then_inc(xc, 1)
                    v.wait_ge(xc, 3 * t + 2)
                    v.tensor_tensor(xt, ex[:], w_res[:], ALU.add).then_inc(x_done, 1)
                    v.wait_ge(x_done, t + 1)
                    settle()
                    v.bn_stats(stats[:, bass.ds(t, 1), :], xs[:, bass.ds(t, 1), :]).then_inc(xc, 1)

                def pair(k, first):
                    for p in range(2):
                        t = 2 * k + p
                        if not (first and p == 0):
                            prepare(t, p, k, first)
                        if not first:
                            elu(t - 2)
                        if not (first and p == 0):
                            combine(t - 1, 1 - p)
                in_pairs(v, pair)
                elu(TILES - 2)
                combine(TILES - 1, 1)
                elu(TILES - 1)

                v.wait_ge(xc, 3 * TILES)
                row_stats(LN_STEPS)
                step = chain(ln, 2 * LN_STEPS)
                step(v.tensor_scalar(rec[:], rowsum[:], 1.0, None, ALU.max))
                step(v.tensor_scalar(farg[:, 0, :], rowsum[:], 0.0, None, ALU.is_gt))
                v.wait_ge(powd, 3)
                step(v.tensor_tensor(dinv[:], dinv[:], farg[:, 0, :], ALU.mult))
                step(v.scalar_tensor_tensor(colx[:, 0, 0, :], rstd[:], SCALE, dinv[:], ALU.mult, ALU.mult))
                step(v.tensor_scalar(dinv[:], dinv[:], 1.0 / SCALE, None, ALU.mult))

                def low1(j, p):
                    v.wait_ge(xhi, 3 * TILES + j + 1)
                    v.scalar_tensor_tensor(x_layer[1][:, bass.ds(j, 1), F:2 * F], ubuf[:, p:p + 1, :],
                                           colx[:, 0, 0, bass.ds(j, 1)], x_layer[1][:, bass.ds(j, 1), 0:F],
                                           ALU.mult, ALU.subtract).then_inc(x_ready[1], 1)
                centred(0, 0, ud)
                centred(1, 1, ud)
                low1(0, 0)
                with v.Fori(1, PAIRS) as k:
                    for p in range(2):
                        j = 2 * k + p
                        v.wait_ge(x_ready[1], j - 1)
                        centred(j, p, ud)
                        low1(j - 1, 1 - p)
                low1(TILES - 1, 1)

                v.tensor_reduce(flags[:, 0:1], bad[:], AX.X, ALU.add).then_inc(flc, 1)
                v.tensor_scalar(farg[:, 0, :], rowsum[:], 0.0, None, ALU.is_le).then_inc(flc, 1)
                v.tensor_scalar(flags[:, 2:3], ext[:, 0:1], ext[:, 1:2], SPREAD - 2.0, ALU.subtract, ALU.is_gt).then_inc(flc, 1)
                step = chain(flc, 3)
                v.wait_ge(flc, 3)
                step(v.tensor_reduce(flags[:, 1:2], farg[:, 0, :], AX.X, ALU.add))
                step(v.tensor_reduce(flags[:, 3:4], flags[:, 0:3], AX.X, ALU.add))
                v.nop().then_inc(flagd, 1)

                for layer in L:
                    def product(t, p):
                        v.wait_ge(mm_done[layer], t + 1)
                        y, z, tl = bank_a[p][:, 0:F], y_sb[:, p, 0:F], tb[:, p * F:(p + 1) * F]
                        v.wait_ge(tl_done[layer], t + 1)
                        if layer == 1:
                            v.scalar_tensor_tensor(z, y, dinv[:, bass.ds(t, 1)], tl, ALU.mult, ALU.add)\
                             .then_inc(z_done[1], 1)
                        else:
                            hi = x_layer[3][:, bass.ds(t, 1), 0:F].rearrange("p a f -> p (a f)")
                            lo = x_layer[3][:, bass.ds(t, 1), F:2 * F].rearrange("p a f -> p (a f)")
                            v.scalar_tensor_tensor(z, y, t_scaled[:], tl, ALU.mult, ALU.add).then_inc(zc[3], 1)
                            v.wait_ge(zc[3], 2 * t + 1)
                            v.scalar_tensor_tensor(z, hi, omt_scaled[:], z, ALU.mult, ALU.add).then_inc(zc[3], 1)
                            v.wait_ge(zc[3], 2 * t + 2)
                            v.scalar_tensor_tensor(z, lo, omt_scaled[:], z, ALU.mult, ALU.add).then_inc(z_done[3], 1)

                    def update(t, p, k, first=False):
                        xt = xs[:, bass.ds(t, 1), :].rearrange("p a f -> p (a f)")
                        o = op[:, 0:F]
                        v.wait_ge(p_done[layer], t + 1)
                        if layer == 1:
                            v.tensor_tensor(w_res[:], o, b_row[:], ALU.add).then_inc(read_o[1], 1)
                            v.wait_ge(read_o[1], t + 1)
                            v.scalar_tensor_tensor(xt, w_res[:], 0.0, xt, ALU.max, ALU.add).then_inc(upd[1], 1)
                            v.wait_ge(upd[1], 3 * t + 1)
                            settle()
                            v.bn_stats(stl[:, p, :], xs[:, bass.ds(t, 1), :]).then_inc(upd[1], 1)
                            v.wait_ge(upd[1], 3 * t + 2)
                            v.tensor_tensor(gm[:], stl[:, p, 1:2], stl[:, p, 4:5], ALU.add).then_inc(upd[1], 1)
                            v.wait_ge(upd[1], 3 * t + 3)
                            v.tensor_scalar(x_layer[2][:, bass.ds(t, 1), 0:F], xs[:, bass.ds(t, 1), :], 2.0, gm[:],
                                            ALU.mult, ALU.is_gt).then_inc(x_ready[2], 1)
                        elif layer == 2:
                            v.scalar_tensor_tensor(xt, o, 0.0, xt, ALU.max, ALU.add).then_inc(read_o[2], 1)
                            v.wait_ge(read_o[2], t + 1)
                            settle()
                            v.bn_stats(stl[:, p, :], xs[:, bass.ds(t, 1), :]).then_inc(upd[2], 1)
                            v.wait_ge(upd[2], t + 1)
                            settle()
                            v.bn_aggr(mv[:, p, :], stl[:, p, :]).then_inc(aggd, 1)
                        else:
                            if not first:
                                v.wait_ge(stored[p], 16 * k)
                            v.tensor_tensor(xo[:, p, :], o, xt, ALU.add).then_inc(upd[3], 1)
                            v.wait_ge(upd[3], t + 1)
                            v.nop().then_inc(read_o[3], 1)

                    def norm(t, p):
                        v.wait_ge(rstdd, t + 1)
                        v.tensor_scalar(ubuf[:, p:p + 1, :], xs[:, bass.ds(t, 1), :], mv[:, p, 0:1], 0.0,
                                        ALU.subtract, ALU.max).then_inc(nrm, 1)
                        v.wait_ge(nrm, 2 * t + 1)
                        v.tensor_scalar(x_layer[3][:, bass.ds(t, 1), 0:F], ubuf[:, p:p + 1, :], cst[:, p:p + 1], None,
                                        ALU.mult).then_inc(nrm, 1)
                        v.wait_ge(nrm, 2 * t + 2)
                        v.scalar_tensor_tensor(x_layer[3][:, bass.ds(t, 1), F:2 * F], ubuf[:, p:p + 1, :], cst[:, p:p + 1],
                                               x_layer[3][:, bass.ds(t, 1), 0:F], ALU.mult, ALU.subtract)\
                         .then_inc(x_ready[3], 1)

                    def pair(k, first):
                        for p in range(2):
                            t = 2 * k + p
                            if layer != 2:
                                product(t, p)
                            if not (first and p == 0):
                                update(t - 1, 1 - p, k if p else k - 1, first)
                            if layer == 2 and not first:
                                norm(t - 2, p)
                    in_pairs(v, pair)
                    if layer == 2:
                        norm(TILES - 2, 0)
                    update(TILES - 1, 1, PAIRS - 1)
                    if layer == 2:
                        norm(TILES - 1, 1)
                    if layer == 1:
                        v.wait_ge(flagd, 2)
                        v.tensor_scalar(general, bank_c[0][0:1, 0:1], NP - N + 0.5, None, ALU.is_gt).then_inc(flagd, 1)


def gnn_program(nc, io):
    with nc.sbuf_tensor("general", [1, 1], I32) as general:
        fast_program(nc, io, general[:])
        found = nc.values_load(general[:], min_val=0, max_val=1)
        with nc.If(found > 0):
            general_program(nc, io)


def kernel(x, adj, L0_gnn_W, L0_gnn_a, L0_gnn_wtrans, L1_gnn_W, L1_gnn_b, L2_gnn_weight, L3_gnn_t, L3_gnn_weight):
    import concourse.bacc as bacc
    from concourse.bass_utils import run_bass_kernel_spmd

    adj_pad = np.pad(np.asarray(adj), ((0, NP - N), (0, NP - N)))
    x_pad = np.pad(np.asarray(x), ((0, NP - N), (0, 0)))
    arrays = {
        "x": np.ascontiguousarray(x_pad.reshape(TILES, P, F).transpose(1, 0, 2)),
        "adj": adj_pad,
        "adj_t": np.ascontiguousarray(
            adj_pad.reshape(TILES, P, TILES, P).transpose(0, 3, 2, 1).reshape(NP, NP)),
        "w_att_t": np.ascontiguousarray(np.asarray(L0_gnn_W).T),
        "a_vec": np.ascontiguousarray(np.asarray(L0_gnn_a).reshape(2 * FB, P).T),
        "wtrans": np.asarray(L0_gnn_wtrans),
        "w1": np.asarray(L1_gnn_W),
        "b1": np.asarray(L1_gnn_b),
        "w2_t": np.ascontiguousarray(np.asarray(L2_gnn_weight).T),
        "t3": np.asarray(L3_gnn_t),
        "w3": np.asarray(L3_gnn_weight),
        "ident": np.eye(P, dtype=np.float32),
    }
    nc = bacc.Bacc("TRN2", target_bir_lowering=False, num_devices=1)
    io = {n: nc.dram_tensor(n + "_dram", a.shape, mybir.dt.from_np(a.dtype), kind="ExternalInput").ap()
          for n, a in arrays.items()}
    io["out"] = nc.dram_tensor("out_dram", (N, F), F32, kind="ExternalOutput").ap()
    gnn_program(nc, io)
    r = run_bass_kernel_spmd(nc, [{n + "_dram": a for n, a in arrays.items()}], core_ids=[0])
    return r.results[0]["out_dram"]
```

```python
from contextlib import ExitStack

import numpy as np
import concourse.bass as bass
from concourse import mybir

P = 128
F32 = mybir.dt.float32
F16 = mybir.dt.float16
F8 = mybir.dt.float8e4
U8 = mybir.dt.uint8
I32 = mybir.dt.int32
ALU = mybir.AluOpType
ACT = mybir.ActivationFunctionType
AX = mybir.AxisListType

N, F = 3327, 256
TILES = -(-N // P)
NP = TILES * P
PAIRS = TILES // 2
FB = F // P
ALPHA = 0.2
MASKED = 1e12
EPS = 1e-5
SPREAD = 10.0
SCALE = 2048.0
TINY = 1e-30
GROUPS = [(g, min(4, TILES - g)) for g in range(0, TILES, 4)]


def general_program(nc, io, prefix="g_"):
    adj, adj_t, w_att_t, a_vec, wtrans, w1, b1, w2_t, t3, w3, out = (
        io[n] for n in ("adj", "adj_t", "w_att_t", "a_vec", "wtrans", "w1", "b1", "w2_t", "t3", "w3", "out"))
    with ExitStack() as ctx:
        def sb(name, shape, dt=F32):
            return ctx.enter_context(nc.sbuf_tensor(prefix + name, shape, dt))

        def ps(name):
            return ctx.enter_context(nc.psum_tensor(prefix + name, [P, 512], F32))

        def sem(name):
            return ctx.enter_context(nc.semaphore(prefix + name))

        xs = sb("xs", [P, TILES, F])
        h = sb("h", [P, TILES, F])
        ident = sb("ident", [P, P])
        ones = sb("ones", [P, P])
        w_att_sb = sb("w_att_sb", [P, FB, F])
        a_sb = sb("a_sb", [P, 2, FB])
        wtrans_sb = sb("wtrans_sb", [P, 2 * FB, F])
        w_sb = {1: sb("w1_sb", [P, FB, F]), 2: sb("w2_sb", [P, FB, F]), 3: sb("w3_sb", [P, FB, F])}
        b_row = sb("b_row", [P, F])
        t_col = sb("t_col", [P, 1])
        omt_col = sb("omt_col", [P, 1])
        wa = sb("wa", [P, 2, F])
        s_col = sb("s_col", [P, TILES])
        t_nodes = sb("t_nodes", [P, TILES])
        t_row = sb("t_row", [P, NP])
        rowsum = sb("rowsum", [P, TILES])
        stats = sb("stats", [P, TILES, 6])
        mean = sb("mean", [P, TILES])
        var = sb("var", [P, TILES])
        rec = sb("rec", [P, TILES])
        rstd = sb("rstd", [P, TILES])
        nwt = sb("nwt", [P, TILES])
        dinv = sb("dinv", [P, TILES])
        diag = sb("diag", [P, 2, P])
        abuf = sb("abuf", [P, 2, NP])
        ebuf = sb("ebuf", [P, NP])
        prob = sb("prob", [P, NP])
        prob_t = sb("prob_t", [P, TILES, P])
        nmax = sb("nmax", [P, 2])
        psums = sb("psums", [P, 2])
        prec = sb("prec", [P, 2])
        y_sb = sb("y_sb", [P, 2 * F])
        yt_sb = sb("yt_sb", [P, 2 * F])
        elu_m = sb("elu_m", [P, F])
        elu_e = sb("elu_e", [P, F])

        tp = [ps(f"tp{i}") for i in range(2)]
        yp = [ps(f"yp{i}") for i in range(2)]
        ep = [ps(f"ep{i}") for i in range(2)]
        op = [ps(f"op{i}") for i in range(2)]

        loaded = sem("loaded")
        prep = sem("prep")
        wa_done = sem("wa_done")
        wa_here = sem("wa_here")
        with nc.Block() as block:
            @block.sync
            def _(sp):
                sp.dma_start(xs[:], io["x"]).then_inc(loaded, 16)
                sp.dma_start(ident[:], io["ident"]).then_inc(loaded, 16)
                sp.dma_start(w_att_sb[:], w_att_t.rearrange("(c p) f -> p c f", p=P)).then_inc(loaded, 16)
                sp.dma_start(a_sb[:], a_vec.rearrange("p (s c) -> p s c", s=2)).then_inc(loaded, 16)
                sp.dma_start(wtrans_sb[:], wtrans.rearrange("(c p) f -> p c f", p=P)).then_inc(loaded, 16)
                for layer, w in ((1, w1), (2, w2_t), (3, w3)):
                    sp.dma_start(w_sb[layer][:], w.rearrange("(c p) f -> p c f", p=P)).then_inc(loaded, 16)

            @block.scalar
            def _(a):
                a.dma_start(b_row[:], b1.rearrange("(a f) -> a f", a=1).broadcast_to([P, F])).then_inc(loaded, 16)
                a.dma_start(t_col[:], t3.rearrange("(a f) -> a f", a=1).broadcast_to([P, 1])).then_inc(loaded, 16)

            @block.gpsimd
            def _(g):
                g.memset(ones[:], 1.0).then_inc(prep, 1)

            @block.vector
            def _(v):
                v.memset(prob[:], 0.0).then_inc(prep, 1)
                v.wait_ge(loaded, 160)
                v.wait_ge(prep, 2)
                rep = prob[:, 0:2 * FB * P].rearrange("p (s c m) -> p s c m", s=2, c=FB)
                for s in range(2):
                    for c in range(FB):
                        v.tensor_scalar(rep[:, s, c, :], ones[:], a_sb[:, s, c:c + 1], None,
                                        ALU.mult).then_inc(prep, 1)
                w2v = w_sb[2][:]
                v.tensor_scalar(h[:, 0:FB, :], w2v, 0.0, None, ALU.is_gt).then_inc(prep, 1)
                v.tensor_scalar(h[:, FB:2 * FB, :], w2v, 0.0, None, ALU.is_lt).then_inc(prep, 1)
                v.wait_ge(prep, 8)
                v.tensor_tensor(w2v, h[:, 0:FB, :], h[:, FB:2 * FB, :], ALU.subtract).then_inc(prep, 1)
                v.tensor_scalar(omt_col[:], t_col[:], -1.0, 1.0, ALU.mult, ALU.add).then_inc(prep, 1)
                v.wait_ge(wa_done, 1)
                v.tensor_copy(wa[:], yp[0][:].rearrange("p (s f) -> p s f", s=2)).then_inc(wa_here, 1)
                v.memset(prob[:, 0:2 * FB * P], 0.0).then_inc(wa_here, 1)

            @block.tensor
            def _(pe):
                pe.wait_ge(prep, 6)
                rep = prob[:, 0:2 * FB * P].rearrange("p (s c m) -> p s c m", s=2, c=FB)
                for s in range(2):
                    for c in range(FB):
                        mm = pe.matmul(yp[0][:, s * F:(s + 1) * F], rep[:, s, c, :], w_att_sb[:, c, :],
                                       start=(c == 0), stop=(c == FB - 1))
                mm.then_inc(wa_done, 1)

        def layer_norm(layer):
            lv = sem(f"ln_v{layer}")
            la = sem(f"ln_a{layer}")
            lp = sem(f"ln_p{layer}")
            with nc.Block() as block:
                @block.vector
                def _(v):
                    with v.Fori(0, TILES) as t:
                        v.bn_stats(stats[:, bass.ds(t, 1), :], xs[:, bass.ds(t, 1), :]).then_inc(lv, 1)
                    n = TILES

                    def step(inst, n):
                        inst.then_inc(lv, 1)
                        v.wait_ge(lv, n + 1)
                        return n + 1
                    v.wait_ge(lv, n)

                    def rsqrt(o, i, roots, n):
                        n = step(v.reciprocal(rec[:], i), n)
                        v.wait_ge(la, roots)
                        n = step(v.tensor_tensor(nwt[:], o, o, ALU.mult), n)
                        n = step(v.tensor_tensor(nwt[:], nwt[:], i, ALU.mult), n)
                        n = step(v.tensor_scalar(nwt[:], nwt[:], -0.5, 1.5, ALU.mult, ALU.add), n)
                        return step(v.tensor_tensor(o, o, nwt[:], ALU.mult), n)
                    n = step(v.tensor_tensor(mean[:], stats[:, :, 1], stats[:, :, 4], ALU.add), n)
                    n = step(v.tensor_scalar(mean[:], mean[:], 0.5, None, ALU.mult), n)
                    n = step(v.tensor_tensor(rec[:], stats[:, :, 1], stats[:, :, 4], ALU.subtract), n)
                    n = step(v.scalar_tensor_tensor(rec[:], rec[:], 0.25, rec[:], ALU.mult, ALU.mult), n)
                    n = step(v.tensor_tensor(var[:], stats[:, :, 2], stats[:, :, 5], ALU.add), n)
                    n = step(v.scalar_tensor_tensor(var[:], var[:], 1.0 / F, rec[:], ALU.mult, ALU.add), n)
                    n = step(v.tensor_scalar(var[:], var[:], EPS, None, ALU.add), n)
                    n = rsqrt(rstd[:], var[:], 1, n)
                    if layer == 1:
                        n = step(v.tensor_scalar(var[:], rowsum[:], 1e-34, None, ALU.max), n)
                        n = rsqrt(dinv[:], var[:], 2, n)
                        n = step(v.tensor_scalar(nwt[:], rowsum[:], 0.0, None, ALU.is_gt), n)
                        n = step(v.tensor_tensor(dinv[:], dinv[:], nwt[:], ALU.mult), n)
                        n = step(v.tensor_tensor(rstd[:], rstd[:], dinv[:], ALU.mult), n)
                    with v.Fori(0, TILES) as t:
                        ht = h[:, bass.ds(t, 1), :]
                        xt = xs[:, bass.ds(t, 1), :]
                        m = mean[:, bass.ds(t, 1)]
                        if layer == 2:
                            v.tensor_scalar(ht, xt, m, None, ALU.is_gt).then_inc(lv, 1)
                        else:
                            v.tensor_scalar(ht, xt, m, 0.0, ALU.subtract, ALU.max).then_inc(lv, 1)
                            v.wait_ge(lv, n + 1 + t * (4 if layer == 0 else 2))
                            v.tensor_scalar(ht, ht, rstd[:, bass.ds(t, 1)], None, ALU.mult).then_inc(lv, 1)
                        if layer == 0:
                            for s, o in enumerate((s_col, t_nodes)):
                                v.wait_ge(lv, n + 2 + s + t * 4)
                                v.scalar_tensor_tensor(ebuf[:, 0:F], h[:, bass.ds(t, 1), :].rearrange("p a f -> p (a f)"),
                                                       1.0, wa[:, s, :], ALU.mult, ALU.mult,
                                                       accum_out=o[:, bass.ds(t, 1)]).then_inc(lv, 1)
                    if layer == 0:
                        n += 4 * TILES
                        for t in range(TILES):
                            v.wait_ge(lv, n)
                            if t >= 2:
                                v.wait_ge(lp, t - 1)
                            v.tensor_scalar(diag[:, t % 2, :], ident[:], t_nodes[:, t:t + 1], None,
                                            ALU.mult).then_inc(la, 1)
                            if t >= 1:
                                v.wait_ge(lp, t)
                                v.tensor_copy(t_row[:, (t - 1) * P:t * P], tp[(t - 1) % 2][:, 0:P]).then_inc(wa_here, 1)
                        v.wait_ge(lp, TILES)
                        v.tensor_copy(t_row[:, (TILES - 1) * P:], tp[(TILES - 1) % 2][:, 0:P]).then_inc(wa_here, 1)

                @block.scalar
                def _(a):
                    n = TILES + 7
                    a.wait_ge(lv, n + 1)
                    a.activation(rstd[:], rec[:], ACT.Sqrt).then_inc(la, 1)
                    if layer == 1:
                        a.wait_ge(lv, n + 7)
                        a.activation(dinv[:], rec[:], ACT.Sqrt).then_inc(la, 1)

                if layer == 0:
                    @block.tensor
                    def _(pe):
                        for t in range(TILES):
                            pe.wait_ge(la, 2 + t)
                            if t >= 2:
                                pe.wait_ge(wa_here, 2 + t - 1)
                            pe.matmul(tp[t % 2][:, 0:P], ones[:], diag[:, t % 2, :],
                                      start=True, stop=True).then_inc(lp, 1)

        layer_norm(0)

        a_here = [sem(f"a_here{p}") for p in range(2)]
        a_free = [sem(f"a_free{p}") for p in range(2)]
        vq = sem("vq")
        expd = sem("expd")
        tpd = sem("tpd")
        tpc = sem("tpc")
        ypd = sem("ypd")
        epd = sem("epd")
        epc = sem("epc")
        opd = sem("opd")
        elu = sem("elu")
        NG = len(GROUPS)
        VT = 17
        with nc.Block() as block:
            @block.sync
            def _(sp):
                with sp.Fori(0, PAIRS) as k:
                    for p in range(2):
                        t = 2 * k + p
                        sp.wait_ge(a_free[p], k + 1)
                        sp.dma_start(abuf[:, p, :], adj[bass.ds(t * P, P), :]).then_inc(a_here[p], 16)

            @block.vector
            def _(v):
                for p in range(2):
                    v.nop().then_inc(a_free[p], 1)
                with v.Fori(0, PAIRS) as k:
                    for p in range(2):
                        t = 2 * k + p
                        base = t * VT
                        ab = abuf[:, p, :]

                        def step(inst, n):
                            inst.then_inc(vq, 1)
                            v.wait_ge(vq, base + n)
                        v.wait_ge(a_here[p], 16 * k + 16)
                        v.tensor_reduce(rowsum[:, bass.ds(t, 1)], ab, AX.X, ALU.add).then_inc(vq, 1)
                        step(v.tensor_scalar(ebuf[:], t_row[:], s_col[:, bass.ds(t, 1)], None, ALU.add), 2)
                        step(v.tensor_scalar(ab, ab, 0.0, None, ALU.is_gt), 3)
                        step(v.scalar_tensor_tensor(ebuf[:], ebuf[:], ALPHA, ebuf[:], ALU.mult, ALU.max), 4)
                        step(v.tensor_tensor(ebuf[:], ebuf[:], ab, ALU.mult), 5)
                        step(v.tensor_scalar(ab, ab, 1.0, MASKED, ALU.subtract, ALU.mult), 6)
                        v.wait_ge(tpd, 1 + 2 * NG * t)
                        step(v.tensor_tensor(prob[:, 0:N], ebuf[:, 0:N], ab[:, 0:N], ALU.add), 7)
                        v.tensor_reduce(nmax[:, 0:1], prob[:, 0:N], AX.X, ALU.max, negate=True).then_inc(vq, 1)
                        v.wait_ge(tpd, 1 + 2 * NG * t + NG)
                        step(v.scalar_tensor_tensor(prob[:, 0:N], ebuf[:, 0:N], -1.0, ab[:, 0:N], ALU.mult, ALU.add), 9)
                        v.tensor_reduce(nmax[:, 1:2], prob[:, 0:N], AX.X, ALU.max, negate=True).then_inc(a_free[p], 1)
                        v.wait_ge(expd, 2 * t + 2)
                        step(v.reciprocal(prec[:], psums[:]), 10)
                        step(v.tensor_scalar(prec[:, 1:2], prec[:, 1:2], -1.0, None, ALU.mult), 11)
                        v.wait_ge(ypd, 1 + 2 * t + 2)
                        for s in range(2):
                            v.tensor_scalar(y_sb[:, s * F:(s + 1) * F], yp[s][:, 0:F], prec[:, s:s + 1], None,
                                            ALU.mult).then_inc(vq, 1)
                        v.wait_ge(opd, t + 1)
                        v.tensor_scalar(elu_m[:], op[0][:, 0:F], 0.0, None, ALU.min).then_inc(vq, 1)
                        v.wait_ge(elu, t + 1)
                        v.tensor_scalar(elu_e[:], elu_e[:], -1.0, None, ALU.add).then_inc(vq, 1)
                        v.wait_ge(vq, base + 15)
                        v.scalar_tensor_tensor(elu_e[:], op[0][:, 0:F], 0.0, elu_e[:], ALU.max, ALU.add).then_inc(vq, 1)
                        v.wait_ge(vq, base + 16)
                        xt = xs[:, bass.ds(t, 1), :].rearrange("p a f -> p (a f)")
                        v.tensor_tensor(xt, xt, elu_e[:], ALU.add).then_inc(vq, 1)

            @block.scalar
            def _(a):
                with a.Fori(0, PAIRS) as k:
                    for p in range(2):
                        t = 2 * k + p
                        for s in range(2):
                            if s == 0:
                                a.wait_ge(vq, VT * t + 8)
                            else:
                                a.wait_ge(a_free[p], k + 2)
                            a.activation(prob[:, 0:N], prob[:, 0:N], ACT.Exp, bias=nmax[:, s:s + 1],
                                         accum_out=psums[:, s:s + 1]).then_inc(expd, 1)
                            for g, (j, n) in enumerate(GROUPS):
                                a.wait_ge(tpd, 1 + (2 * t + s) * NG + g + 1)
                                if g == 0:
                                    a.wait_ge(ypd, 1 + 2 * t + s)
                                a.activation(prob_t[:, j:j + n, :], tp[(s * NG + g) % 2][:, 0:n * P].rearrange("p (j i) -> p j i", j=n), ACT.Copy)\
                                 .then_inc(tpc, 1)
                        a.wait_ge(epd, t + 1)
                        a.activation(yt_sb[:], ep[0][:], ACT.Copy).then_inc(epc, 1)
                        a.wait_ge(vq, VT * t + 14)
                        a.activation(elu_e[:], elu_m[:], ACT.Exp).then_inc(elu, 1)

            @block.tensor
            def _(pe):
                pe.nop().then_inc(tpd, 1)
                pe.nop().then_inc(ypd, 1)
                with pe.Fori(0, PAIRS) as k:
                    for p in range(2):
                        t = 2 * k + p
                        for s in range(2):
                            pe.wait_ge(expd, 2 * t + s + 1)
                            for g, (j, n) in enumerate(GROUPS):
                                q = (2 * p + s) * NG + g
                                if q >= 2:
                                    pe.wait_ge(tpc, 4 * NG * k + q - 1)
                                for i in range(n):
                                    tr = pe.transpose(tp[(s * NG + g) % 2][:, i * P:(i + 1) * P],
                                                      prob[:, (j + i) * P:(j + i + 1) * P], ident[:])
                                tr.then_inc(tpd, 1)
                            pe.wait_ge(tpc, (2 * t + s + 1) * NG)
                            for j in range(TILES):
                                mm = pe.matmul(yp[s][:, 0:F], prob_t[:, j, :], h[:, j, :],
                                               start=(j == 0), stop=(j == TILES - 1))
                            mm.then_inc(ypd, 1)
                        pe.wait_ge(vq, VT * t + 13)
                        for c in range(2 * FB):
                            tr = pe.transpose(ep[0][:, c * P:(c + 1) * P], y_sb[:, c * P:(c + 1) * P], ident[:])
                        tr.then_inc(epd, 1)
                        pe.wait_ge(epc, t + 1)
                        for c in range(2 * FB):
                            mm = pe.matmul(op[0][:, 0:F], yt_sb[:, c * P:(c + 1) * P], wtrans_sb[:, c, :],
                                           start=(c == 0), stop=(c == 2 * FB - 1))
                        mm.then_inc(opd, 1)

        def graph_layer(layer):
            b_here = [sem(f"b_here{layer}_{p}") for p in range(2)]
            y_done = [sem(f"y_done{layer}_{p}") for p in range(2)]
            y_here = [sem(f"y_here{layer}_{p}") for p in range(2)]
            z_done = sem(f"z_done{layer}")
            zt_done = sem(f"zt_done{layer}")
            zt_here = sem(f"zt_here{layer}")
            o_done = sem(f"o_done{layer}")
            v_done = sem(f"v_done{layer}")
            with nc.Block() as block:
                @block.sync
                def _(sp):
                    with sp.Fori(0, PAIRS) as k:
                        for p in range(2):
                            t = 2 * k + p
                            sp.wait_ge(y_done[p], k + 1)
                            sp.dma_start(abuf[:, p, :], adj_t[bass.ds(t * P, P), :]).then_inc(b_here[p], 16)

                @block.tensor
                def _(pe):
                    for p in range(2):
                        pe.nop().then_inc(y_done[p], 1)
                    with pe.Fori(0, PAIRS) as k:
                        for p in range(2):
                            t = 2 * k + p
                            pe.wait_ge(b_here[p], 16 * k + 16)
                            pe.wait_ge(y_here[p], k + 1)
                            for j in range(TILES):
                                mm = pe.matmul(yp[p][:, 0:F], abuf[:, p, j * P:(j + 1) * P], h[:, j, :],
                                               start=(j == 0), stop=(j == TILES - 1))
                            mm.then_inc(y_done[p], 1)
                            pe.wait_ge(z_done, t + 1)
                            for c in range(FB):
                                tr = pe.transpose(ep[p][:, c * P:(c + 1) * P], y_sb[:, p * F + c * P:p * F + (c + 1) * P], ident[:])
                            tr.then_inc(zt_done, 1)
                            pe.wait_ge(zt_here, t + 1)
                            for c in range(FB):
                                mm = pe.matmul(op[p][:, 0:F], yt_sb[:, p * F + c * P:p * F + (c + 1) * P], w_sb[layer][:, c, :],
                                               start=(c == 0), stop=(c == FB - 1))
                            mm.then_inc(o_done, 1)

                @block.scalar
                def _(a):
                    with a.Fori(0, PAIRS) as k:
                        for p in range(2):
                            t = 2 * k + p
                            a.wait_ge(zt_done, t + 1)
                            a.activation(yt_sb[:, p * F:(p + 1) * F], ep[p][:, 0:F], ACT.Copy).then_inc(zt_here, 1)

                @block.vector
                def _(v):
                    for p in range(2):
                        v.nop().then_inc(y_here[p], 1)
                    with v.Fori(0, PAIRS) as k:
                        for p in range(2):
                            t = 2 * k + p
                            y, z = yp[p][:, 0:F], y_sb[:, p * F:(p + 1) * F]
                            xt = xs[:, bass.ds(t, 1), :].rearrange("p a f -> p (a f)")
                            ht = h[:, bass.ds(t, 1), :].rearrange("p a f -> p (a f)")
                            v.wait_ge(y_done[p], k + 2)
                            if layer == 1:
                                v.tensor_scalar(z, y, dinv[:, bass.ds(t, 1)], None, ALU.mult).then_inc(z_done, 1)
                                v.nop().then_inc(y_here[p], 1)
                            elif layer == 2:
                                v.tensor_copy(z, y).then_inc(z_done, 1)
                                v.nop().then_inc(y_here[p], 1)
                            else:
                                v.tensor_scalar(elu_m[:], y, t_col[:], None, ALU.mult).then_inc(y_here[p], 1)
                                v.wait_ge(y_here[p], k + 2)
                                v.scalar_tensor_tensor(z, ht, omt_col[:], elu_m[:], ALU.mult, ALU.add).then_inc(z_done, 1)
                            v.wait_ge(o_done, t + 1)
                            if layer == 1:
                                v.tensor_tensor(elu_e[:], op[p][:, 0:F], b_row[:], ALU.add).then_inc(v_done, 1)
                                v.wait_ge(v_done, 2 * t + 1)
                                v.scalar_tensor_tensor(xt, elu_e[:], 0.0, xt, ALU.max, ALU.add).then_inc(v_done, 1)
                            elif layer == 2:
                                v.scalar_tensor_tensor(xt, op[p][:, 0:F], 0.0, xt, ALU.max, ALU.add).then_inc(v_done, 1)
                            else:
                                v.tensor_tensor(xt, op[p][:, 0:F], xt, ALU.add).then_inc(v_done, 1)

        for layer in (1, 2, 3):
            layer_norm(layer)
            graph_layer(layer)

        stored = sem("stored")
        with nc.Block() as block:
            @block.sync
            def _(sp):
                full = (TILES - 1) * P
                sp.dma_start(out[0:full, :].rearrange("(t p) f -> p t f", p=P), xs[:, 0:TILES - 1, :]).then_inc(stored, 16)
                sp.dma_start(out[full:N, :], xs[0:N - full, TILES - 1, :]).then_inc(stored, 16)
                sp.wait_ge(stored, 32)


def fast_program(nc, io, general, prefix="f_"):
    with ExitStack() as ctx:
        def sb(name, shape, dt=F32):
            return ctx.enter_context(nc.sbuf_tensor(prefix + name, shape, dt))

        def sem(name):
            return ctx.enter_context(nc.semaphore(prefix + name))

        HALF = TILES // 2
        HW = HALF * P
        UB = 4

        xs = sb("xs", [P, TILES, F])
        ident = sb("ident", [P, P])
        ones = sb("ones", [P, P])
        w_att_sb = sb("w_att_sb", [P, FB, F])
        a_sb = sb("a_sb", [P, 2, FB])
        wtrans_sb = sb("wtrans_sb", [P, 2 * FB, F])
        w_sb = {l: sb(f"w{l}_sb", [P, FB, F]) for l in (1, 2, 3)}
        b_row = sb("b_row", [P, F])
        t_col = sb("t_col", [P, 1])
        t_scaled = sb("t_scaled", [P, 1])
        omt_scaled = sb("omt_scaled", [P, 1])
        wa = sb("wa", [P, FB, 2])
        dots = sb("dots", [P, TILES, 2])
        xh = {(g, part): sb(f"x{g}_{part}", [P, TILES, 2 * F], F16) for g in range(2) for part in range(2)}
        x_layer = {1: xh[0, 0], 2: xh[0, 1], 3: xh[1, 0]}
        first_scores = xh[1, 1][:].rearrange("p j c -> p (j c)").bitcast(F32).rearrange("p (q c) -> p q c", q=4)
        late = xh[1, 1][:].rearrange("p j c -> p (j c)")
        sign_w = late[:, 0:FB * F].rearrange("p (c f) -> p c f", c=FB)
        ident16 = late[:, FB * F:FB * F + P]
        binary = late[:, 2 * FB * F:2 * FB * F + 2 * F].rearrange("p (r f) -> p r f", r=2)
        binary_t = late[:, 4 * FB * F:4 * FB * F + F]
        dcol = sb("dcol", [P, TILES, 2, 5], F16)
        adj32 = sb("adj32", [P, 2, HW])
        a8 = sb("a8", [P, 2, NP], F8)
        a8_pair = adj32[:].rearrange("p r c -> p (r c)").bitcast(F8).rearrange("p (r w c) -> p r w c", r=2, w=2)
        above = sb("above", [P, 2, NP], F8)
        below = sb("below", [P, 2, NP], F8)
        wa_rows = above[:].rearrange("p r c -> p (r c)").bitcast(F32)[:, 0:2 * F].rearrange("p (s f) -> p s f", s=2)
        score = sb("score", [P, HW])
        s_tile = sb("s_tile", [P, 2, P])
        s_col = sb("s_col", [P, TILES])
        t_nodes = sb("t_nodes", [P, TILES])
        s_rows = sb("s_rows", [TILES, P])
        ext = sb("ext", [P, 2])
        colf = sb("colf", [P, 2, 2, TILES])
        colx = sb("colx", [P, 2, 2, TILES])
        fac = sb("fac", [P, TILES, 4])
        farg = sb("farg", [P, 4, TILES])
        stats = sb("stats", [P, TILES, 6])
        mean = sb("mean", [P, TILES])
        neg_mean = sb("neg_mean", [P, TILES])
        apart = sb("apart", [P, TILES])
        base = sb("base", [P, 2, TILES])
        root = sb("root", [P, 2, TILES])
        dinv, rstd = root[:, 0, :], root[:, 1, :]
        rowsum = sb("rowsum", [P, TILES])
        has_one = sb("has_one", [P, TILES])
        minus_half = sb("minus_half", [P, 2, TILES])
        bad = sb("bad", [P, 2 * TILES])
        flags = sb("flags", [P, 4])
        ubuf = sb("ubuf", [P, UB, F])
        csb = sb("csb", [P, 2, 5])
        dsum = sb("dsum", [P, 4])
        den = sb("den", [P, 2])
        rfac = sb("rfac", [P, 2, 4])
        tb = sb("tb", [P, 2 * F])
        y_sb = sb("y_sb", [P, 2, 2 * F])
        quad = y_sb[:].rearrange("p r (b f) -> p (r b) f", b=2)
        yt_sb = sb("yt_sb", [P, 2 * F])
        ex = sb("ex", [P, F])
        w_res = sb("w_res", [P, F])
        mv = sb("mv", [P, 2, 2])
        cst = sb("cst", [P, 2])
        xo = sb("xo", [P, 2, F])
        gv = sb("gv", [P, 2])
        gm = sb("gm", [P, 1])
        stl = sb("stl", [P, 2, 6])

        def ps(name):
            return ctx.enter_context(nc.psum_tensor(prefix + name, [P, 512], F32))
        bank_a = [ps(f"bank_a{p}") for p in range(2)]
        bank_b = [ps(f"bank_b{p}") for p in range(2)]
        bank_c = [ps(f"bank_c{p}") for p in range(2)]
        ep, op = ps("ep"), ps("op")

        a8_dram = nc.dram_tensor(prefix + "a8_dram", (TILES, P, NP), U8).ap()
        s_dram = nc.dram_tensor(prefix + "s_dram", (TILES, P), F32).ap()
        adj_t = io["adj_t"]

        always = sem("always")
        waited = sem("waited")
        x_here = [sem(f"x_here{c}") for c in range(4)]
        w_here = sem("w_here")
        late_here = sem("late_here")
        ln = sem("ln")
        lnv = sem("lnv")
        powd = sem("powd")
        wa_done = sem("wa_done")
        mean_done = sem("mean_done")
        cen = sem("cen")
        turned_x = sem("turned_x")
        copied_x = sem("copied_x")
        dot = sem("dot")
        dve_dot = sem("dve_dot")
        rep_done = sem("rep_done")
        half_main = sem("half_main")
        pool_score = sem("pool_score")
        freed = sem("freed")
        dotd = sem("dotd")
        st_done = sem("st_done")
        s_stored = sem("s_stored")
        extd = sem("extd")
        expd = sem("expd")
        xlo = sem("xlo")
        xhi = sem("xhi")
        ud = sem("ud")
        adj_here = [sem(f"adj_here{i}") for i in range(2)]
        s_here = [sem(f"s_here{i}") for i in range(2)]
        cast_done = sem("cast_done")
        check_done = sem("check_done")
        a8_stored = [sem(f"a8_stored{i}") for i in range(2)]
        score_done = sem("score_done")
        masks_done = sem("masks_done")
        main_done = sem("main_done")
        small = sem("small")
        tb_done = sem("tb_done")
        y_done = sem("y_done")
        yt_psum = sem("yt_psum")
        yt_done = sem("yt_done")
        o_done = sem("o_done")
        ex_done = sem("ex_done")
        x_done = sem("x_done")
        xc = sem("xc")
        L = (1, 2, 3)
        pair_here = {(l, r): sem(f"pair_here{l}{r}") for l in L for r in range(2)}
        mm_done = {l: sem(f"mm_done{l}") for l in L}
        tl_done = {l: sem(f"tl_done{l}") for l in L}
        zc = {l: sem(f"zc{l}") for l in L}
        z_done = {l: sem(f"z_done{l}") for l in L}
        zt_psum = {l: sem(f"zt_psum{l}") for l in L}
        zt_done = {l: sem(f"zt_done{l}") for l in L}
        p_done = {l: sem(f"p_done{l}") for l in L}
        upd = {l: sem(f"upd{l}") for l in L}
        read_o = {l: sem(f"read_o{l}") for l in L}
        scale_done = sem("scale_done")
        x_ready = {l: sem(f"x_ready{l}") for l in L}
        signs = sem("signs")
        binary_done = sem("binary_done")
        bt_psum = sem("bt_psum")
        bt_done = sem("bt_done")
        xw_psum = sem("xw_psum")
        aggd = sem("aggd")
        nrm = sem("nrm")
        rstdd = sem("rstdd")
        stored = [sem(f"stored{p}") for p in range(2)]
        flagd = sem("flagd")
        flc = sem("flc")
        vp = sem("vp")
        vst = sem("vst")
        vs = sem("vs")
        xhp = sem("xhp")
        wready = sem("wready")
        gs = sem("gs")

        XCH = [(0, 6), (6, 14), (14, 20), (20, 26)]
        X1_RUNS = [(0, 10), (10, 14), (14, TILES - 2), (TILES - 2, TILES - 1), (TILES - 1, TILES)]
        LN0 = [(0, XCH[2][1]), (XCH[2][1], TILES)]
        LN1 = [(0, TILES - 2), (TILES - 2, TILES - 1), (TILES - 1, TILES)]
        A_STEPS = 7

        UB_ROUNDS = TILES // UB
        WA_COPIED = 3
        EPILOGUE_AT = {1: (9, 15), 3: (13, 19)}
        PE_PAIRS = [0, 1, 3, 4, 7, 8, 10]
        DVE_PAIRS = [m for m in range(PAIRS) if m not in PE_PAIRS]

        def pair_slots(m):
            buffer, n = (quad, PE_PAIRS.index(m)) if m in PE_PAIRS else (ubuf[:], DVE_PAIRS.index(m))
            return buffer[:, 2 * (n % 2):2 * (n % 2) + 2, :]

        def add_scores(eng, o, p, hf):
            tj = t_nodes[:, hf * HALF:(hf + 1) * HALF].rearrange("p (j a) -> p j a", a=1).broadcast_to([P, HALF, P])
            si = s_tile[:, p:p + 1, :].broadcast_to([P, HALF, P])
            return eng.tensor_tensor(o.rearrange("p (j i) -> p j i", j=HALF), tj, si, ALU.add)

        def in_pairs(eng, pair):
            pair(0, True)
            with eng.Fori(1, PAIRS) as k:
                pair(k, False)

        with nc.Block() as block:
            @block.sync
            def _(sp):
                def wait(signal, value):
                    sp.wait_ge(signal, value)
                    if not isinstance(value, int):
                        sp.sem_inc(waited, 1)

                for c, (j0, j1) in enumerate(XCH):
                    sp.dma_start(xs[:, j0:j1, :], io["x"][:, j0:j1, :]).then_inc(x_here[c], 16)

                def load_half(t, hf):
                    sp.dma_start(adj32[:, hf, :], adj_t[bass.ds(t * P, P), hf * HW:(hf + 1) * HW])\
                      .then_inc(adj_here[hf], 16)

                def load_s(t, p):
                    sp.dma_start(s_tile[:, p, :], s_dram[bass.ds(t, 1), :].broadcast_to([P, P])).then_inc(s_here[p], 16)

                def pair(k, first):
                    for p in range(2):
                        t = 2 * k + p
                        for hf in range(2):
                            if not (first and p == 0):
                                wait(cast_done, 2 * t + hf - 1)
                                wait(check_done, 2 * t + hf - 1)
                            load_half(t, hf)
                        if first and p == 0:
                            wait(st_done, 2)
                            sp.dma_start(s_dram, s_rows[:]).then_inc(s_stored, 16)
                            wait(s_stored, 16)
                            load_s(0, 0)
                            load_s(1, 1)
                        if not first:
                            wait(score_done, 2 * t - 2)
                            load_s(t, p)
                        if not (first and p == 0):
                            wait(cast_done, 2 * t)
                            sp.dma_start(a8_dram[bass.ds(t - 1, 1), :, :].rearrange("a p c -> p (a c)"),
                                         a8[:, 1 - p, :].bitcast(U8)).then_inc(a8_stored[1 - p], 16)
                in_pairs(sp, pair)
                wait(cast_done, 2 * TILES)
                sp.dma_start(a8_dram[TILES - 1], a8[:, 1, :].bitcast(U8)).then_inc(a8_stored[1], 16)

                wait(check_done, 2 * TILES)
                for p in range(2):
                    wait(a8_stored[p], 16 * PAIRS)

                def load_pair(layer, q, r):
                    sp.dma_start(a8_pair[:, r].bitcast(U8),
                                 a8_dram[bass.ds(2 * q, 2), :, :].rearrange("w p c -> p w c"))\
                      .then_inc(pair_here[layer, r], 16)

                def store(q, last=False):
                    for p in range(2):
                        t = 2 * q + p
                        wait(upd[3], t + 1)
                        rows = N - (TILES - 1) * P if last and p else P
                        sp.dma_start(io["out"][bass.ds(t * P, rows), :], xo[0:rows, p, :]).then_inc(stored[p], 16)

                for layer in L:
                    def next_pair(q, r, load=True):
                        wait(mm_done[layer], 2 * q + 2)
                        load_pair(layer, q + 2, r)

                    r0 = layer % 2 ^ 1
                    if layer > 1:
                        wait(mm_done[layer - 1], TILES - 2)
                    load_pair(layer, 0, r0)
                    if layer > 1:
                        wait(mm_done[layer - 1], TILES)
                    load_pair(layer, 1, r0 ^ 1)
                    with sp.Fori(0, (PAIRS - 3) // 2) as k:
                        for i in range(2):
                            next_pair(2 * k + i, r0 ^ i)
                            if layer == 3:
                                store(2 * k + i)
                    next_pair(PAIRS - 3, r0)
                    if layer == 3:
                        for q in range(PAIRS - 3, PAIRS):
                            store(q, q == PAIRS - 1)
                for p in range(2):
                    wait(stored[p], 16 * PAIRS)

            @block.gpsimd
            def _(g):
                g.memset(minus_half[:], -0.5).then_inc(always, 1)
                g.wait_ge(always, 1)

                def inverse_root(lo, hi, which, turn):
                    g.wait_ge(ln, turn)
                    g.tensor_tensor(root[:, which, lo:hi], base[:, which, lo:hi], minus_half[:, which, lo:hi], ALU.pow)\
                     .then_inc(powd, 1)
                for n, (lo, hi) in enumerate(LN0):
                    inverse_root(lo, hi, slice(1, 2), n + 1)

                g.wait_ge(extd, 2)
                for t in range(2):
                    g.wait_ge(s_here[t], 16)
                    for hf in range(2):
                        add_scores(g, first_scores[:, 2 * t + hf, :], t, hf).then_inc(pool_score, 1)

                def x0_block(j, p):
                    g.wait_ge(ud, j + 1)
                    g.sem_inc(waited, 1)
                    for side in range(2):
                        g.tensor_tensor(xh[1, 0][:, bass.ds(j, 1), side * F:(side + 1) * F], ubuf[:, p:p + 1, :],
                                        colx[:, 1, side:side + 1, bass.ds(j, 1)].broadcast_to([P, 1, F]), ALU.mult)\
                         .then_inc(xhp, 1)
                with g.Fori(0, UB_ROUNDS) as k:
                    for p in range(UB):
                        x0_block(UB * k + p, p)
                for j in range(UB * UB_ROUNDS, TILES):
                    x0_block(j, j % UB)
                for n, (lo, hi) in enumerate(LN1):
                    inverse_root(lo, hi, slice(0, 2), len(LN0) + n + 1)

                with g.Fori(0, PAIRS) as k:
                    for p in range(2):
                        t = 2 * k + p
                        g.wait_ge(aggd, t + 1)
                        g.sem_inc(waited, 1)
                        g.tensor_scalar(gv[:, p:p + 1], mv[:, p, 1:2], EPS, None, ALU.add).then_inc(gs, 1)
                        g.wait_ge(gs, 2 * t + 1)
                        g.sem_inc(waited, 1)
                        g.tensor_tensor(gv[:, p:p + 1], gv[:, p:p + 1], minus_half[:, 0, 0:1], ALU.pow).then_inc(gs, 1)
                        g.wait_ge(gs, 2 * t + 2)
                        g.sem_inc(waited, 1)
                        g.tensor_scalar(cst[:, p:p + 1], gv[:, p:p + 1], SCALE, None, ALU.mult).then_inc(rstdd, 1)

            @block.scalar
            def _(a):
                def settle():
                    a.sem_inc(waited, 1)
                a.dma_start(w_att_sb[:], io["w_att_t"].rearrange("(c p) f -> p c f", p=P)).then_inc(w_here, 16)
                a.dma_start(a_sb[:], io["a_vec"].rearrange("p (s c) -> p s c", s=2)).then_inc(w_here, 16)
                a.dma_start(ident[:], io["ident"]).then_inc(w_here, 16)
                a.dma_start(wtrans_sb[:], io["wtrans"].rearrange("(c p) f -> p c f", p=P)).then_inc(late_here, 16)
                for layer, w in ((1, "w1"), (2, "w2_t"), (3, "w3")):
                    a.dma_start(w_sb[layer][:], io[w].rearrange("(c p) f -> p c f", p=P)).then_inc(late_here, 16)
                a.dma_start(b_row[:], io["b1"].rearrange("(a f) -> a f", a=1).broadcast_to([P, F])).then_inc(late_here, 16)
                a.dma_start(t_col[:], io["t3"].rearrange("(a f) -> a f", a=1).broadcast_to([P, 1])).then_inc(late_here, 16)

                def cast(t, p, k, hf):
                    a.wait_ge(adj_here[hf], 16 * t + 16)
                    if hf == 0 and k is not None:
                        a.wait_ge(a8_stored[p], 16 * k)
                        a.wait_ge(masks_done, 4 * t - 4)
                    settle()
                    a.activation(a8[:, p, hf * HW:(hf + 1) * HW], adj32[:, hf, :], ACT.Copy, saturate=False)\
                     .then_inc(cast_done, 1)

                def centre(block, p, done):
                    a.activation(ubuf[:, p:p + 1, :], xs[:, block, :], ACT.Relu, bias=neg_mean[:, block]).then_inc(done, 1)

                def copy_turned(m):
                    if m in PE_PAIRS:
                        n = PE_PAIRS.index(m)
                        a.wait_ge(turned_x, n + 1)
                        if n >= 2:
                            a.wait_ge(dot, n - 1)
                        a.activation((tb, yt_sb)[n % 2][:], (ep, bank_a[0])[n % 2][:], ACT.Copy).then_inc(copied_x, 1)

                for c, (j0, j1) in enumerate(XCH):
                    a.wait_ge(mean_done, c + 1)
                    for m in range(j0 // 2, j1 // 2):
                        if m in PE_PAIRS[2:]:
                            a.wait_ge(turned_x, PE_PAIRS.index(m) - 1)
                        if m in DVE_PAIRS[2:]:
                            a.wait_ge(dve_dot, 4 * DVE_PAIRS.index(m) - 4)
                        for b in range(2):
                            j = 2 * m + b
                            a.activation(pair_slots(m)[:, b, :], xs[:, j, :], ACT.Relu, bias=neg_mean[:, j:j + 1])\
                             .then_inc(cen, 1)
                        if m > j0 // 2:
                            copy_turned(m - 1)
                    copy_turned(j1 // 2 - 1)
                    if c == 0:
                        a.wait_ge(wa_done, 2)
                        a.activation(wa_rows.rearrange("p s f -> p (s f)"), bank_b[0][:], ACT.Copy).then_inc(wa_done, 1)

                a.wait_ge(st_done, 1)
                a.activation(s_rows[:], ep[0:TILES, 0:P], ACT.Copy).then_inc(st_done, 1)
                cast(0, 0, None, 0)
                cast(0, 0, None, 1)
                a.wait_ge(extd, 2)
                a.activation(colf[:], colx[:], ACT.Exp).then_inc(expd, 1)
                cast(1, 1, None, 0)
                cast(1, 1, None, 1)

                def x0_high(j, p):
                    a.wait_ge(ud, j + 1)
                    for s in range(2):
                        a.activation(xh[0, 0][:, bass.ds(j, 1), s * F:(s + 1) * F], ubuf[:, p:p + 1, :], ACT.Copy,
                                     scale=colx[:, 0, s, bass.ds(j, 1)]).then_inc(xhi, 1)
                a.wait_ge(expd, 2)
                centre(bass.ds(0, 1), 0, ud)
                for j in range(1, UB):
                    centre(bass.ds(j, 1), j, ud)
                    x0_high(j - 1, j - 1)

                def x0_step(j, p):
                    a.wait_ge(xlo, 4 * (j - UB) + 4)
                    settle()
                    centre(bass.ds(j, 1), p, ud)
                    x0_high(j - 1, (p - 1) % UB)
                with a.Fori(1, UB_ROUNDS) as k:
                    for p in range(UB):
                        x0_step(UB * k + p, p)
                for j in range(UB * UB_ROUNDS, TILES):
                    x0_step(j, j % UB)
                x0_high(TILES - 1, (TILES - 1) % UB)
                a.wait_ge(extd, 3)
                a.activation(fac[:].rearrange("p t g -> p g t"), farg[:], ACT.Exp).then_inc(expd, 1)

                def turn_copy(t):
                    a.wait_ge(yt_psum, t + 1)
                    a.activation(yt_sb[:], ep[:], ACT.Copy).then_inc(yt_done, 1)

                def elu_exp(t):
                    a.wait_ge(o_done, t + 1)
                    if not isinstance(t, int) or t > 0:
                        a.wait_ge(x_done, t)
                    a.activation(ex[:], op[:, 0:F], ACT.Exp).then_inc(ex_done, 1)

                def below_part(t, p):
                    a.wait_ge(small, A_STEPS * t + A_STEPS)
                    for s in range(2):
                        a.activation(tb[:, s * F:(s + 1) * F], bank_b[p][:, s * F:(s + 1) * F], ACT.Copy,
                                     scale=rfac[:, p, 2 + s:3 + s]).then_inc(tb_done, 1)

                def steady(t, p, k, last=False):
                    cast(t, p, k, 1)
                    turn_copy(t - 2)
                    elu_exp(t - 2)
                    below_part(t - 1, 1 - p)
                    if not last:
                        cast(t + 1, 1 - p, k if p == 0 else k + 1, 0)
                cast(2, 0, 1, 0)
                below_part(0, 0)
                with a.Fori(1, PAIRS - 1) as k:
                    for p in range(2):
                        steady(2 * k + p, p, k)
                for p in range(2):
                    steady(TILES - 2 + p, p, PAIRS - 1, p == 1)
                def x1_run(run):
                    lo, hi = X1_RUNS[run]
                    if run in (0, 3, 4):
                        a.wait_ge(scale_done, 1 + max(0, run - 2))
                    for j in range(lo, hi + 1):
                        if j < hi:
                            if j >= UB:
                                a.wait_ge(x_ready[1], j - UB + 1)
                            else:
                                a.wait_ge(wready, 1)
                            centre(slice(j, j + 1), j % UB, ud)
                        if j > lo:
                            b = j - 1
                            a.wait_ge(ud, TILES + b + 1)
                            a.wait_ge(freed, b + 1)
                            a.activation(x_layer[1][:, b:b + 1, 0:F], ubuf[:, b % UB:b % UB + 1, :], ACT.Copy,
                                         scale=colx[:, 0, 0, b:b + 1]).then_inc(xhi, 1)
                x1_run(0)
                turn_copy(TILES - 2)
                x1_run(1)
                elu_exp(TILES - 2)
                x1_run(2)
                x1_run(3)
                below_part(TILES - 1, 1)
                turn_copy(TILES - 1)
                elu_exp(TILES - 1)
                x1_run(4)

                for layer in (1, 3):
                    def product(t, p):
                        a.wait_ge(mm_done[layer], t + 1)
                        scale = dinv[:, bass.ds(t, 1)] if layer == 1 else t_scaled[:]
                        a.activation(tb[:, p * F:(p + 1) * F], bank_a[p][:, F:2 * F], ACT.Copy,
                                     scale=scale).then_inc(tl_done[layer], 1)

                    def sign_product(t):
                        a.wait_ge(bt_psum, t + 1)
                        a.activation(binary_t, bank_b[0][:, 0:F], ACT.Copy).then_inc(bt_done, 1)
                        a.wait_ge(xw_psum, t + 1)
                        settle()
                        a.activation(x_layer[2][:, bass.ds(t, 1), 0:F], bank_b[1][:, 0:F].rearrange("p (a f) -> p a f", a=1),
                                     ACT.Copy).then_inc(x_ready[2], 1)

                    def turned(t):
                        a.wait_ge(zt_psum[layer], t + 1)
                        a.activation(yt_sb[:, 0:F], ep[:, 0:F], ACT.Copy).then_inc(zt_done[layer], 1)

                    def pair(k, first):
                        for p in range(2):
                            t = 2 * k + p
                            if layer == 1 and not first:
                                sign_product(t - 2)
                            if not (first and p == 0):
                                turned(t - 1)
                            product(t, p)
                    in_pairs(a, pair)
                    if layer == 1:
                        sign_product(TILES - 2)
                    turned(TILES - 1)
                    if layer == 1:
                        sign_product(TILES - 1)

            @block.tensor
            def _(pe):
                def settle():
                    pe.sem_inc(waited, 1)
                pe.wait_ge(vp, 1)
                with pe.Fori(0, 12):
                    for _ in range(2):
                        pe.matmul(bank_b[0][:, 0:P], ones[:], ones[:], start=True, stop=True)
                pe.wait_ge(w_here, 48)
                for f in range(FB):
                    for c in range(FB):
                        mm = pe.matmul(bank_c[0][:, 2 * f:2 * f + 2], w_att_sb[:, c, f * P:(f + 1) * P], a_sb[:, :, c],
                                       start=(c == 0), stop=(c == FB - 1))
                mm.then_inc(wa_done, 1)
                def turn_pair(n):
                    m = PE_PAIRS[n]
                    pe.wait_ge(cen, 2 * m + 2)
                    if n >= 2:
                        pe.wait_ge(copied_x, n - 1)
                    for c in range(2 * FB):
                        tr = pe.transpose((ep, bank_a[0])[n % 2][:, c * P:(c + 1) * P],
                                          pair_slots(m)[:, c // FB, c % FB * P:(c % FB + 1) * P], ident[:])
                    tr.then_inc(turned_x, 1)

                def multiply_pair(n):
                    m = PE_PAIRS[n]
                    pe.wait_ge(copied_x, n + 1)
                    for b in range(2):
                        j = 2 * m + b
                        for c in range(FB):
                            at = (b * FB + c) * P
                            mm = pe.matmul(op[:, 2 * j:2 * j + 2], (tb, yt_sb)[n % 2][:, at:at + P], wa[:, c, :],
                                           start=(c == 0), stop=(c == FB - 1))
                    mm.then_inc(dot, 1)

                turn_pair(0)
                pe.wait_ge(rep_done, 4)
                rep = score[:, 0:2 * FB * P].rearrange("p (s c m) -> p s c m", s=2, c=FB)
                for s in range(2):
                    for c in range(FB):
                        mm = pe.matmul(bank_b[0][:, s * F:(s + 1) * F], rep[:, s, c, :], w_att_sb[:, c, :],
                                       start=(c == 0), stop=(c == FB - 1))
                mm.then_inc(wa_done, 1)
                pe.wait_ge(vp, WA_COPIED)
                for n in range(1, len(PE_PAIRS)):
                    turn_pair(n)
                    multiply_pair(n - 1)
                multiply_pair(len(PE_PAIRS) - 1)
                pe.wait_ge(dotd, 1)
                pe.transpose(ep[0:TILES, 0:P], s_col[:], ident[:]).then_inc(st_done, 1)
                pe.wait_ge(dotd, 6)
                pe.matmul(op[:, 0:2 * P], ones[:], y_sb[:, 0, 0:2 * P], start=True, stop=True).then_inc(extd, 1)

                def turn(t, p, done, ready, blocks, per=1):
                    pe.wait_ge(ready, per * t + per)
                    for c in range(blocks):
                        tr = pe.transpose(ep[:, c * P:(c + 1) * P], y_sb[:, p, c * P:(c + 1) * P], ident[:])
                    tr.then_inc(done, 1)

                def project(t, w, blocks, turned, done):
                    pe.wait_ge(turned, t + 1)
                    for c in range(blocks):
                        mm = pe.matmul(op[:, 0:F], yt_sb[:, c * P:(c + 1) * P], w[:, c, :],
                                       start=(c == 0), stop=(c == blocks - 1))
                    mm.then_inc(done, 1)

                def attention_epilogue(t, p, part, first=False):
                    if part == 0:
                        turn(t, p, yt_psum, y_done, 2 * FB, 2)
                    else:
                        if first:
                            pe.wait_ge(late_here, 16 * 6)
                        else:
                            pe.wait_ge(xc, 3 * t - 1)
                            pe.wait_ge(ex_done, t)
                        project(t, wtrans_sb, 2 * FB, yt_done, o_done)

                def main_block(p, j, last=False):
                    lo, hi = j * P, (j + 1) * P
                    for g, (mask, bank) in enumerate(((above, bank_a[p]), (below, bank_b[p]))):
                        mm = pe.matmul(bank[:], mask[:, p, lo:hi], xh[g, 0][:, j, :], start=(j == 0), stop=False)
                        if last and g == 0:
                            mm.then_inc(freed, 1)
                        pe.matmul(bank[:], mask[:, p, lo:hi], xh[g, 1][:, j, :], start=False, stop=(j == TILES - 1))
                        mm = pe.matmul(bank_c[p][:, 5 * g:5 * g + 5], mask[:, p, lo:hi], dcol[:, j, g, :],
                                       start=(j == 0 and g == 0), stop=(j == TILES - 1), skip_group_check=True)
                    return mm

                def main(t, p, epilogues, last=False):
                    for j in range(TILES):
                        if j % HALF == 0:
                            pe.wait_ge(masks_done, 4 * t + 2 * (j // HALF) + 2)
                            if j == 0:
                                pe.wait_ge(y_done, 2 * t - 2)
                            settle()
                        if j in epilogues:
                            back, part, first = epilogues[j]
                            attention_epilogue(t - back, p if back == 2 else 1 - p, part, first)
                        mm = main_block(p, j, last)
                    mm.then_inc(main_done, 1)

                pe.wait_ge(masks_done, 8)
                for j in range(TILES):
                    pe.wait_ge(xlo, 4 * j + 4)
                    for p in range(2):
                        mm = main_block(p, j)
                        if j == TILES - 1:
                            mm.then_inc(main_done, 1)
                        elif j == HALF - 1 and p == 0:
                            mm.then_inc(half_main, 1)
                main(2, 0, {4: (2, 0, False), 9: (2, 1, True), 16: (1, 0, False), 21: (1, 1, False)})
                steady = {8: (1, 0, False), 14: (1, 1, False)}
                main(3, 1, steady)
                with pe.Fori(2, PAIRS - 1) as k:
                    for p in range(2):
                        main(2 * k + p, p, steady)
                for p in range(2):
                    main(TILES - 2 + p, p, steady, p == 1)

                def layer_epilogue(layer, t, p, part, first=False):
                    if part == 0:
                        turn(t, p, zt_psum[layer], z_done[layer], FB)
                    else:
                        if first:
                            pe.wait_ge(x_done if layer == 1 else read_o[1], TILES)
                        else:
                            pe.wait_ge(read_o[layer], t)
                        project(t, w_sb[layer], FB, zt_done[layer], p_done[layer])

                def sign_turn(t, p):
                    pe.wait_ge(binary_done, t + 1)
                    for c in range(FB):
                        mm = pe.matmul(bank_b[0][:, c * P:(c + 1) * P], binary[:, p, c * P:(c + 1) * P], ident16,
                                       start=True, stop=True)
                    mm.then_inc(bt_psum, 1)

                def sign_multiply(t):
                    pe.wait_ge(bt_done, t + 1)
                    for c in range(FB):
                        mm = pe.matmul(bank_b[1][:, 0:F], binary_t[:, c * P:(c + 1) * P], sign_w[:, c, :],
                                       start=(c == 0), stop=(c == FB - 1))
                    mm.then_inc(xw_psum, 1)

                for layer in L:
                    W = F if layer == 2 else 2 * F
                    r0 = layer % 2 ^ 1

                    def block(j, p, r):
                        return pe.matmul(bank_a[p][:, 0:W], a8_pair[:, r, p, j * P:(j + 1) * P], x_layer[layer][:, j, 0:W],
                                         start=(j == 0), stop=(j == TILES - 1))

                    def tile(q, p, r, n):
                        t = 2 * q + p
                        if p == 0:
                            pe.wait_ge(pair_here[layer, r], n)
                        pe.wait_ge(z_done[layer], t - 1)
                        settle()
                        for j in range(TILES):
                            if layer == 1 and j == 2:
                                sign_turn(t - 2, p)
                            if layer == 1 and j == 6:
                                sign_multiply(t - 2)
                            if layer != 2 and j in EPILOGUE_AT[layer]:
                                layer_epilogue(layer, t - 1, 1 - p, EPILOGUE_AT[layer].index(j))
                            mm = block(j, p, r)
                        mm.then_inc(mm_done[layer], 1)

                    held = 2 if layer == 2 else 1
                    pe.wait_ge(pair_here[layer, r0], 16)
                    for p in range(2):
                        if layer == 1:
                            pe.wait_ge(y_done, 2 * TILES - 2 + 2 * p)
                        else:
                            pe.wait_ge(z_done[layer - 1], TILES - 1 + p)
                        for j in range(TILES - held):
                            if layer == 1 and (p, j) in ((0, 18), (1, 4)):
                                attention_epilogue(TILES - 1, 1, p)
                            if layer == 2 and (p, j) == (0, 6):
                                sign_turn(TILES - 2, 0)
                            if layer == 2 and (p, j) == (0, 12):
                                sign_multiply(TILES - 2)
                            if layer == 2 and (p, j) in ((0, 16), (1, 0)):
                                layer_epilogue(1, TILES - 1, 1, p)
                            if p == 0:
                                pe.wait_ge(x_ready[layer], j + 1)
                            block(j, p, r0)
                    if layer == 2:
                        sign_turn(TILES - 1, 1)
                        sign_multiply(TILES - 1)
                    pe.wait_ge(x_ready[layer], TILES)
                    for p in range(2):
                        for j in range(TILES - held, TILES):
                            mm = block(j, p, r0)
                        mm.then_inc(mm_done[layer], 1)
                    if layer != 2:
                        layer_epilogue(layer, 0, 0, 0)
                        layer_epilogue(layer, 0, 0, 1, True)
                    with pe.Fori(0, PAIRS // 2) as k:
                        for i in range(2):
                            q = 2 * k + 1 + i
                            for p in range(2):
                                tile(q, p, r0 ^ 1 ^ i, 16 * k + 16 + 16 * i)
                    if layer == 1:
                        pe.wait_ge(flagd, 1)
                        pe.matmul(bank_c[0][:, 0:1], ones[:], flags[:, 3:4], start=True, stop=True).then_inc(flagd, 1)

                for part in range(2):
                    layer_epilogue(3, TILES - 1, 1, part)

            @block.vector
            def _(v):
                def settle():
                    v.sem_inc(waited, 1)
                v.memset(ones[:], 1.0).then_inc(vp, 1)
                v.memset(dcol[:], 1.0).then_inc(vp, 1)

                def chain(sem, n):
                    count = [n]

                    def step(inst):
                        inst.then_inc(sem, 1)
                        count[0] += 1
                        v.wait_ge(sem, count[0])
                    return step

                def means(step, lo, hi):
                    step(v.tensor_tensor(mean[:, lo:hi], stats[:, lo:hi, 1], stats[:, lo:hi, 4], ALU.add))
                    step(v.tensor_scalar(neg_mean[:, lo:hi], mean[:, lo:hi], -0.5, None, ALU.mult))

                def variances(step, lo, hi):
                    far, var = apart[:, lo:hi], base[:, 1, lo:hi]
                    step(v.tensor_tensor(far, stats[:, lo:hi, 1], stats[:, lo:hi, 4], ALU.subtract))
                    step(v.scalar_tensor_tensor(far, far, 0.25, far, ALU.mult, ALU.mult))
                    step(v.tensor_tensor(var, stats[:, lo:hi, 2], stats[:, lo:hi, 5], ALU.add))
                    step(v.scalar_tensor_tensor(var, var, 1.0 / F, far, ALU.mult, ALU.add))
                    v.tensor_scalar(var, var, EPS, None, ALU.add).then_inc(ln, 1)

                def dot_products(m):
                    for b in range(2):
                        v.wait_ge(cen, 2 * m + b + 1)
                        for s in range(2):
                            n = 4 * DVE_PAIRS.index(m) + 2 * b + s
                            if n >= 2:
                                v.wait_ge(dve_dot, n - 1)
                            v.scalar_tensor_tensor((ex, w_res)[s][:], pair_slots(m)[:, b, :], 1.0, wa_rows[:, s, :],
                                                   ALU.mult, ALU.mult, accum_out=dots[:, 2 * m + b, s:s + 1])\
                             .then_inc(dve_dot, 1)

                stat_step = chain(vs, 0)
                for c, (j0, j1) in enumerate(XCH):
                    v.wait_ge(x_here[c], 16)
                    for j in range(j0, j1):
                        v.bn_stats(stats[:, j, :], xs[:, j, :]).then_inc(vst, 1)
                    v.wait_ge(vst, j1)
                    means(stat_step, j0, j1)
                    v.nop().then_inc(mean_done, 1)
                    if c == 0:
                        v.wait_ge(w_here, 48)
                        v.wait_ge(vp, 1)
                        rep = score[:, 0:2 * FB * P].rearrange("p (s c m) -> p s c m", s=2, c=FB)
                        for s in range(2):
                            for f in range(FB):
                                v.tensor_scalar(rep[:, s, f, :], ones[:], a_sb[:, s, f:f + 1], None, ALU.mult)\
                                 .then_inc(rep_done, 1)
                        v.wait_ge(wa_done, 1)
                        v.tensor_copy(wa[:], bank_c[0][:, 0:2 * FB].rearrange("p (c s) -> p c s", s=2)).then_inc(vp, 1)
                    if c == 1:
                        v.wait_ge(wa_done, 3)
                    if c >= 2:
                        variances(stat_step, *LN0[c - 2])
                    for m in DVE_PAIRS:
                        if c > 0 and XCH[c - 1][0] <= 2 * m < XCH[c - 1][1]:
                            dot_products(m)
                for m in DVE_PAIRS:
                    if 2 * m >= XCH[-1][0]:
                        dot_products(m)

                v.wait_ge(dot, len(PE_PAIRS))
                for m in PE_PAIRS:
                    v.tensor_copy(dots[:, 2 * m:2 * m + 2, :], op[:, 4 * m:4 * m + 4].rearrange("p (j s) -> p j s", s=2))\
                     .then_inc(dve_dot, 1)
                v.wait_ge(dve_dot, 4 * len(DVE_PAIRS) + len(PE_PAIRS))
                v.wait_ge(powd, 2)
                v.tensor_tensor(s_col[:], dots[:, :, 0], rstd, ALU.mult).then_inc(dotd, 1)
                step = chain(dotd, 1)
                step(v.tensor_tensor(t_nodes[:], dots[:, :, 1], rstd, ALU.mult))
                step(v.tensor_reduce(ext[:, 0:1], t_nodes[:], AX.X, ALU.max))
                step(v.tensor_reduce(ext[:, 1:2], t_nodes[:], AX.X, ALU.min))
                step(v.tensor_scalar(y_sb[:, 0, 0:P], ident[:], ext[:, 0:1], None, ALU.mult))
                step(v.tensor_scalar(y_sb[:, 0, P:2 * P], ident[:], ext[:, 1:2], None, ALU.mult))
                v.wait_ge(extd, 1)
                step(v.tensor_reduce(ext[:, 0:1], op[:, 0:P], AX.X, ALU.max))
                step(v.tensor_reduce(ext[:, 1:2], op[:, P:2 * P], AX.X, ALU.min))
                for g, rate in enumerate((1.0, ALPHA)):
                    step(v.tensor_scalar(colx[:, g, 0, :], t_nodes[:], ext[:, 0:1], rate, ALU.subtract, ALU.mult))
                    last = v.tensor_scalar(colx[:, g, 1, :], t_nodes[:], ext[:, 1:2], -rate, ALU.subtract, ALU.mult)
                    if g == 0:
                        step(last)
                last.then_inc(extd, 1)
                v.wait_ge(expd, 1)
                step(v.tensor_scalar(colx[:], colf[:], SCALE, None, ALU.mult))
                cview = colx[:].rearrange("p g s t -> p t g s")
                v.wait_ge(vp, WA_COPIED)
                step(v.tensor_copy(dcol[:, :, :, 0:2], cview))
                step(v.tensor_tensor(dcol[:, :, :, 2:4], cview, dcol[:, :, :, 0:2], ALU.subtract))
                step(v.tensor_tensor(colx[:].rearrange("p g s t -> p (g s) t"), colx[:].rearrange("p g s t -> p (g s) t"),
                                     rstd.rearrange("p (a t) -> p a t", a=1).broadcast_to([P, 4, TILES]), ALU.mult))
                v.nop().then_inc(expd, 1)

                def split_adj(t, p, hf, scores):
                    part = slice(hf * HW, (hf + 1) * HW)
                    v.scalar_tensor_tensor(above[:, p, part], scores, 0.0, a8[:, p, part], ALU.is_gt, ALU.mult,
                                           saturate=False).then_inc(masks_done, 1)
                    v.scalar_tensor_tensor(below[:, p, part], scores, 0.0, a8[:, p, part], ALU.is_le, ALU.mult,
                                           saturate=False).then_inc(masks_done, 1)

                def check_adj(q, hf):
                    a32 = adj32[:, hf, :]
                    v.scalar_tensor_tensor(score[:], a32, 0.0, a32, ALU.is_gt, ALU.not_equal,
                                           accum_out=bad[:, bass.ds(q, 1)]).then_inc(check_done, 1)

                def prepare(t, p, k, hf, masks_free=None):
                    q = 2 * t + hf
                    v.wait_ge(adj_here[hf], 16 * t + 16)
                    v.wait_ge(masks_done, 2 * q)
                    check_adj(q, hf)
                    v.wait_ge(check_done, q + 1)
                    if hf == 0:
                        v.wait_ge(s_here[p], 16 * k + 16)
                    add_scores(v, score[:], p, hf).then_inc(score_done, 1)
                    v.wait_ge(score_done, q + 1)
                    v.wait_ge(cast_done, q + 1)
                    if masks_free:
                        v.wait_ge(*masks_free)
                    elif hf == 0:
                        v.wait_ge(main_done, t - 1)
                    settle()
                    split_adj(t, p, hf, score[:])

                for t in range(2):
                    for hf in range(2):
                        q = 2 * t + hf
                        v.wait_ge(adj_here[hf], 16 * t + 16)
                        if q:
                            v.wait_ge(check_done, q)
                        check_adj(q, hf)
                        v.wait_ge(pool_score, q + 1)
                        v.nop().then_inc(score_done, 1)
                        v.wait_ge(cast_done, q + 1)
                        split_adj(t, t, hf, first_scores[:, q, :])
                v.wait_ge(masks_done, 8)

                def low_parts(j, p):
                    for g in range(2):
                        for side in range(2):
                            v.wait_ge((xhi, xhp)[g], 2 * j + side + 1)
                            cols = slice(side * F, (side + 1) * F)
                            v.scalar_tensor_tensor(xh[g, 1][:, bass.ds(j, 1), cols], ubuf[:, p:p + 1, :],
                                                   colx[:, g, side, bass.ds(j, 1)], xh[g, 0][:, bass.ds(j, 1), cols],
                                                   ALU.mult, ALU.subtract).then_inc(xlo, 1)
                with v.Fori(0, UB_ROUNDS) as k:
                    for p in range(UB):
                        low_parts(UB * k + p, p)
                for j in range(UB * UB_ROUNDS, TILES):
                    low_parts(j, j % UB)

                gap = 1.0 - ALPHA
                step(v.tensor_scalar(farg[:, 0, :], s_col[:], ext[:, 0:1], gap, ALU.add, ALU.mult))
                step(v.tensor_scalar(farg[:, 1, :], s_col[:], ext[:, 1:2], -gap, ALU.add, ALU.mult))
                step(v.tensor_scalar(farg[:, 2, :], farg[:, 0, :], -1.0, 0.0, ALU.mult, ALU.min))
                step(v.tensor_scalar(farg[:, 0, :], farg[:, 0, :], 0.0, None, ALU.min))
                step(v.tensor_scalar(farg[:, 3, :], farg[:, 1, :], -1.0, 0.0, ALU.mult, ALU.max))
                step(v.tensor_scalar(farg[:, 1, :], farg[:, 1, :], 0.0, SPREAD - 1.0, ALU.max, ALU.min))
                v.tensor_scalar(farg[:, 3, :], farg[:, 3, :], SPREAD - 1.0, None, ALU.min).then_inc(extd, 1)
                v.wait_ge(late_here, 96)
                v.wait_ge(xlo, 4 * TILES)
                w2v = w_sb[2][:]
                scr = ubuf[:, 0:FB, :]
                step(v.tensor_scalar(scr, w2v, 0.0, None, ALU.is_gt))
                step(v.tensor_scalar(w2v, w2v, 0.0, None, ALU.is_lt))
                step(v.tensor_tensor(w2v, scr, w2v, ALU.subtract))
                step(v.tensor_scalar(wtrans_sb[:, FB:2 * FB, :], wtrans_sb[:, FB:2 * FB, :], -1.0, None, ALU.mult))
                step(v.tensor_scalar(t_scaled[:], t_col[:], 1.0 / SCALE, None, ALU.mult))
                v.tensor_scalar(omt_scaled[:], t_col[:], -1.0 / SCALE, 1.0 / SCALE, ALU.mult, ALU.add).then_inc(wready, 1)

                def combine(t, p):
                    n = A_STEPS * t
                    v.wait_ge(main_done, t + 1)
                    cs = csb[:]
                    v.tensor_copy(cs, bank_c[p][:, 0:10].rearrange("p (g c) -> p g c", g=2)).then_inc(small, 1)
                    v.wait_ge(small, n + 1)
                    v.tensor_tensor(dsum[:].rearrange("p (g s) -> p g s", g=2), csb[:, :, 0:2], csb[:, :, 2:4], ALU.add).then_inc(small, 1)
                    v.tensor_tensor(rowsum[:, bass.ds(t, 1)], csb[:, 0, 4:5], csb[:, 1, 4:5], ALU.add).then_inc(small, 1)
                    v.wait_ge(small, n + 2)
                    f = fac[:, bass.ds(t, 1), :].rearrange("p a g -> p (a g)")
                    v.tensor_tensor(dsum[:], dsum[:], f, ALU.mult).then_inc(small, 1)
                    v.wait_ge(small, n + 4)
                    v.scalar_tensor_tensor(den[:], dsum[:, 0:2], TINY, dsum[:, 2:4], ALU.max, ALU.add).then_inc(small, 1)
                    v.wait_ge(small, n + 5)
                    v.reciprocal(den[:], den[:]).then_inc(small, 1)
                    v.wait_ge(small, n + 6)
                    v.tensor_tensor(rfac[:, p, :].rearrange("p (g s) -> p g s", g=2), f.rearrange("p (g s) -> p g s", g=2),
                                    den[:].rearrange("p (a s) -> p a s", a=1).broadcast_to([P, 2, 2]), ALU.mult).then_inc(small, 1)
                    v.wait_ge(small, n + 7)
                    for s in range(2):
                        v.wait_ge(tb_done, 2 * t + s + 1)
                        cols = slice(s * F, (s + 1) * F)
                        v.scalar_tensor_tensor(y_sb[:, p, cols], bank_a[p][:, cols], rfac[:, p, s:s + 1], tb[:, cols],
                                               ALU.mult, ALU.add).then_inc(y_done, 1)

                def elu(t):
                    xt = xs[:, bass.ds(t, 1), :].rearrange("p a f -> p (a f)")
                    v.wait_ge(ex_done, t + 1)
                    v.scalar_tensor_tensor(w_res[:], op[:, 0:F], 0.0, xt, ALU.max, ALU.add).then_inc(xc, 1)
                    v.tensor_scalar(ex[:], ex[:], 1.0, -1.0, ALU.min, ALU.add).then_inc(xc, 1)
                    v.wait_ge(xc, 3 * t + 2)
                    v.tensor_tensor(xt, ex[:], w_res[:], ALU.add).then_inc(x_done, 1)
                    v.wait_ge(x_done, t + 1)
                    settle()
                    v.bn_stats(stats[:, bass.ds(t, 1), :], xs[:, bass.ds(t, 1), :]).then_inc(xc, 1)

                ln_step = chain(lnv, 0)

                def row_sizes(run):
                    lo, hi = LN1[run]
                    means(ln_step, lo, hi)
                    ln_step(v.tensor_scalar(base[:, 0, lo:hi], rowsum[:, lo:hi], 1.0, None, ALU.max))
                    ln_step(v.tensor_scalar(has_one[:, lo:hi], rowsum[:, lo:hi], 0.0, 1.0 / SCALE, ALU.is_gt, ALU.mult))
                    variances(ln_step, lo, hi)

                def row_scales(run):
                    lo, hi = LN1[run]
                    v.wait_ge(powd, len(LN0) + run + 1)
                    ln_step(v.tensor_tensor(dinv[:, lo:hi], dinv[:, lo:hi], has_one[:, lo:hi], ALU.mult))
                    v.scalar_tensor_tensor(colx[:, 0, 0, lo:hi], rstd[:, lo:hi], SCALE * SCALE, dinv[:, lo:hi],
                                           ALU.mult, ALU.mult).then_inc(scale_done, 1)
                    v.wait_ge(scale_done, run + 1)

                def low1(lo, hi):
                    for j in range(lo, hi):
                        v.wait_ge(xhi, 2 * TILES + j + 1)
                        v.scalar_tensor_tensor(x_layer[1][:, j:j + 1, F:2 * F], ubuf[:, j % UB:j % UB + 1, :],
                                               colx[:, 0, 0, j:j + 1], x_layer[1][:, j:j + 1, 0:F],
                                               ALU.mult, ALU.subtract).then_inc(x_ready[1], 1)

                v.wait_ge(expd, 3)
                v.wait_ge(check_done, 4)
                prepare(2, 0, 1, 0, (half_main, 1))
                combine(0, 0)

                def steady(t, p, k):
                    prepare(t, p, k, 1)
                    elu(t - 2)
                    combine(t - 1, 1 - p)
                    prepare(t + 1, 1 - p, k if p == 0 else k + 1, 0)
                with v.Fori(1, PAIRS - 1) as k:
                    for p in range(2):
                        steady(2 * k + p, p, k)
                steady(TILES - 2, 0, PAIRS - 1)
                prepare(TILES - 1, 1, PAIRS - 1, 1)
                elu(TILES - 3)
                v.wait_ge(xc, 3 * (TILES - 2))
                row_sizes(0)
                combine(TILES - 2, 0)
                row_scales(0)
                low1(0, X1_RUNS[1][1])
                elu(TILES - 2)
                v.wait_ge(xc, 3 * (TILES - 1))
                row_sizes(1)
                low1(*X1_RUNS[2])
                row_scales(1)
                low1(*X1_RUNS[3])
                combine(TILES - 1, 1)
                elu(TILES - 1)
                v.wait_ge(xc, 3 * TILES)
                row_sizes(2)
                row_scales(2)
                low1(*X1_RUNS[4])

                v.tensor_copy(sign_w, w_sb[2][:]).then_inc(signs, 1)
                v.tensor_copy(ident16, ident[:]).then_inc(signs, 1)
                v.wait_ge(signs, 2)

                v.tensor_reduce(flags[:, 0:1], bad[:], AX.X, ALU.add).then_inc(flc, 1)
                v.tensor_scalar(farg[:, 0, :], rowsum[:], 0.0, None, ALU.is_le).then_inc(flc, 1)
                v.tensor_scalar(flags[:, 2:3], ext[:, 0:1], ext[:, 1:2], SPREAD - 2.0, ALU.subtract, ALU.is_gt).then_inc(flc, 1)
                step = chain(flc, 3)
                v.wait_ge(flc, 3)
                step(v.tensor_reduce(flags[:, 1:2], farg[:, 0, :], AX.X, ALU.add))
                step(v.tensor_reduce(flags[:, 3:4], flags[:, 0:3], AX.X, ALU.add))
                v.nop().then_inc(flagd, 1)

                for layer in L:
                    def product(t, p):
                        v.wait_ge(mm_done[layer], t + 1)
                        y, z, tl = bank_a[p][:, 0:F], y_sb[:, p, 0:F], tb[:, p * F:(p + 1) * F]
                        v.wait_ge(tl_done[layer], t + 1)
                        if layer == 1:
                            v.scalar_tensor_tensor(z, y, dinv[:, bass.ds(t, 1)], tl, ALU.mult, ALU.add)\
                             .then_inc(z_done[1], 1)
                        else:
                            hi = x_layer[3][:, bass.ds(t, 1), 0:F].rearrange("p a f -> p (a f)")
                            lo = x_layer[3][:, bass.ds(t, 1), F:2 * F].rearrange("p a f -> p (a f)")
                            v.scalar_tensor_tensor(z, y, t_scaled[:], tl, ALU.mult, ALU.add).then_inc(zc[3], 1)
                            v.wait_ge(zc[3], 2 * t + 1)
                            v.scalar_tensor_tensor(z, hi, omt_scaled[:], z, ALU.mult, ALU.add).then_inc(zc[3], 1)
                            v.wait_ge(zc[3], 2 * t + 2)
                            v.scalar_tensor_tensor(z, lo, omt_scaled[:], z, ALU.mult, ALU.add).then_inc(z_done[3], 1)

                    def update(t, p, k, first=False):
                        xt = xs[:, bass.ds(t, 1), :].rearrange("p a f -> p (a f)")
                        o = bank_a[p][:, 0:F] if layer == 2 else op[:, 0:F]
                        v.wait_ge(mm_done[2] if layer == 2 else p_done[layer], t + 1)
                        if layer == 1:
                            v.tensor_tensor(w_res[:], o, b_row[:], ALU.add).then_inc(read_o[1], 1)
                            v.wait_ge(read_o[1], t + 1)
                            v.scalar_tensor_tensor(xt, w_res[:], 0.0, xt, ALU.max, ALU.add).then_inc(upd[1], 1)
                            v.wait_ge(upd[1], 3 * t + 1)
                            settle()
                            v.bn_stats(stl[:, p, :], xs[:, bass.ds(t, 1), :]).then_inc(upd[1], 1)
                            v.wait_ge(upd[1], 3 * t + 2)
                            v.tensor_tensor(gm[:], stl[:, p, 1:2], stl[:, p, 4:5], ALU.add).then_inc(upd[1], 1)
                            v.wait_ge(upd[1], 3 * t + 3)
                            settle()
                            v.tensor_scalar(binary[:, p:p + 1, :], xs[:, bass.ds(t, 1), :], 2.0, gm[:],
                                            ALU.mult, ALU.is_gt).then_inc(binary_done, 1)
                        elif layer == 2:
                            v.scalar_tensor_tensor(xt, o, 0.0, xt, ALU.max, ALU.add).then_inc(z_done[2], 1)
                            v.wait_ge(z_done[2], t + 1)
                            settle()
                            v.bn_stats(stl[:, p, :], xs[:, bass.ds(t, 1), :]).then_inc(upd[2], 1)
                            v.wait_ge(upd[2], t + 1)
                            settle()
                            v.bn_aggr(mv[:, p, :], stl[:, p, :]).then_inc(aggd, 1)
                        else:
                            if not first:
                                v.wait_ge(stored[p], 16 * k)
                            v.tensor_tensor(xo[:, p, :], o, xt, ALU.add).then_inc(upd[3], 1)
                            v.wait_ge(upd[3], t + 1)
                            v.nop().then_inc(read_o[3], 1)

                    def norm(t, p):
                        v.wait_ge(rstdd, t + 1)
                        v.tensor_scalar(ubuf[:, p:p + 1, :], xs[:, bass.ds(t, 1), :], mv[:, p, 0:1], 0.0,
                                        ALU.subtract, ALU.max).then_inc(nrm, 1)
                        v.wait_ge(nrm, 2 * t + 1)
                        v.tensor_scalar(x_layer[3][:, bass.ds(t, 1), 0:F], ubuf[:, p:p + 1, :], cst[:, p:p + 1], None,
                                        ALU.mult).then_inc(nrm, 1)
                        v.wait_ge(nrm, 2 * t + 2)
                        v.scalar_tensor_tensor(x_layer[3][:, bass.ds(t, 1), F:2 * F], ubuf[:, p:p + 1, :], cst[:, p:p + 1],
                                               x_layer[3][:, bass.ds(t, 1), 0:F], ALU.mult, ALU.subtract)\
                         .then_inc(x_ready[3], 1)

                    def pair(k, first):
                        for p in range(2):
                            t = 2 * k + p
                            if layer == 2:
                                update(t, p, k)
                                if not (first and p == 0):
                                    norm(t - 1, 1 - p)
                                continue
                            if layer == 3:
                                product(t, p)
                            if not (first and p == 0):
                                update(t - 1, 1 - p, k if p else k - 1, first)
                            if layer == 1:
                                product(t, p)
                    if layer == 1:
                        product(0, 0)
                        product(1, 1)
                        update(0, 0, 0, True)
                        with v.Fori(1, PAIRS) as k:
                            pair(k, False)
                    else:
                        in_pairs(v, pair)
                    if layer == 2:
                        norm(TILES - 1, 1)
                    else:
                        update(TILES - 1, 1, PAIRS - 1)
                    if layer == 1:
                        v.wait_ge(flagd, 2)
                        v.tensor_scalar(general, bank_c[0][0:1, 0:1], NP - N + 0.5, None, ALU.is_gt).then_inc(flagd, 1)


def gnn_program(nc, io):
    with nc.sbuf_tensor("general", [1, 1], I32) as general:
        fast_program(nc, io, general[:])
        found = nc.values_load(general[:], min_val=0, max_val=1)
        with nc.If(found > 0):
            general_program(nc, io)


def kernel(x, adj, L0_gnn_W, L0_gnn_a, L0_gnn_wtrans, L1_gnn_W, L1_gnn_b, L2_gnn_weight, L3_gnn_t, L3_gnn_weight):
    import concourse.bacc as bacc
    from concourse.bass_utils import run_bass_kernel_spmd

    adj_pad = np.pad(np.asarray(adj), ((0, NP - N), (0, NP - N)))
    x_pad = np.pad(np.asarray(x), ((0, NP - N), (0, 0)))
    arrays = {
        "x": np.ascontiguousarray(x_pad.reshape(TILES, P, F).transpose(1, 0, 2)),
        "adj": adj_pad,
        "adj_t": np.ascontiguousarray(
            adj_pad.reshape(TILES, P, TILES, P).transpose(0, 3, 2, 1).reshape(NP, NP)),
        "w_att_t": np.ascontiguousarray(np.asarray(L0_gnn_W).T),
        "a_vec": np.ascontiguousarray(np.asarray(L0_gnn_a).reshape(2 * FB, P).T),
        "wtrans": np.asarray(L0_gnn_wtrans),
        "w1": np.asarray(L1_gnn_W),
        "b1": np.asarray(L1_gnn_b),
        "w2_t": np.ascontiguousarray(np.asarray(L2_gnn_weight).T),
        "t3": np.asarray(L3_gnn_t),
        "w3": np.asarray(L3_gnn_weight),
        "ident": np.eye(P, dtype=np.float32),
    }
    nc = bacc.Bacc("TRN2", target_bir_lowering=False, num_devices=1)
    io = {n: nc.dram_tensor(n + "_dram", a.shape, mybir.dt.from_np(a.dtype), kind="ExternalInput").ap()
          for n, a in arrays.items()}
    io["out"] = nc.dram_tensor("out_dram", (N, F), F32, kind="ExternalOutput").ap()
    gnn_program(nc, io)
    r = run_bass_kernel_spmd(nc, [{n + "_dram": a for n, a in arrays.items()}], core_ids=[0])
    return r.results[0]["out_dram"]
```
